# Optimizing a Trainium2 kernel written in Bass

```python
import numpy as np
import jax
import jax.numpy as jnp

def _softmax(x, axis=-1):
    return jax.nn.softmax(x, axis=axis)

def _gelu(x):
    return jax.nn.gelu(x, approximate=True)

def _silu(x):
    return jax.nn.silu(x)

def _sigmoid(x):
    return jax.nn.sigmoid(x)

def _layernorm(x, axis=-1, eps=1e-05):
    m = jnp.mean(x, axis=axis, keepdims=True)
    v = jnp.var(x, axis=axis, keepdims=True)
    return (x - m) / jnp.sqrt(v + eps)

def _scatter_add(tgt, idx, src, axis=0):
    return tgt.at[idx].add(src)

def _segment_sum(src, seg, n):
    return jax.ops.segment_sum(src, seg, n)
kernel_name = 'mk_hybrid_d1_jaxref_r8_991441'

def setup_inputs(seed: int=0):
    np.random.seed(seed)
    _w = jnp.asarray

    def _L0_attn_a_setup():
        import jax, jax.numpy as jnp
        import numpy as np
        B, S, E = (4, 512, 128)
        CHUNK = 32
        key = jax.random.key(seed)
        ks = jax.random.split(key, 9)
        sd = 1.0 / np.sqrt(E)
        x = jax.random.normal(ks[0], (B, S, E), dtype=jnp.float32)
        Wq = jax.random.normal(ks[1], (E, E), dtype=jnp.float32) * sd
        Wk = jax.random.normal(ks[2], (E, E), dtype=jnp.float32) * sd
        Wv = jax.random.normal(ks[3], (E, E), dtype=jnp.float32) * sd
        Wo = jax.random.normal(ks[4], (E, E), dtype=jnp.float32) * sd
        bq = jax.random.normal(ks[5], (E,), dtype=jnp.float32) * 0.01
        bk = jax.random.normal(ks[6], (E,), dtype=jnp.float32) * 0.01
        bv = jax.random.normal(ks[7], (E,), dtype=jnp.float32) * 0.01
        bo = jax.random.normal(ks[8], (E,), dtype=jnp.float32) * 0.01
        return {'x': x, 'Wq': Wq, 'bq': bq, 'Wk': Wk, 'bk': bk, 'Wv': Wv, 'bv': bv, 'Wo': Wo, 'bo': bo}
    _L0_attn_a_in = _L0_attn_a_setup()

    def _L0_attn_b_setup():
        import jax, jax.numpy as jnp
        import numpy as np
        EMBED_DIM = 128
        NUM_HEADS = 16
        HEAD_DIM = EMBED_DIM // NUM_HEADS
        BATCH = 2
        SEQ = 256
        key = jax.random.key(seed)
        k1, k2, k3, k4, k5 = jax.random.split(key, 5)
        scale_in = 1.0 / np.sqrt(EMBED_DIM)
        return {'x': jax.random.normal(k1, (BATCH, SEQ, EMBED_DIM), dtype=jnp.float32), 'head_mask': jnp.ones((NUM_HEADS,), dtype=jnp.float32), 'qkv_w': jax.random.normal(k2, (3 * EMBED_DIM, EMBED_DIM), dtype=jnp.float32) * scale_in, 'qkv_b': jax.random.normal(k3, (3 * EMBED_DIM,), dtype=jnp.float32) * 0.02, 'fc_w': jax.random.normal(k4, (EMBED_DIM, EMBED_DIM), dtype=jnp.float32) * scale_in, 'fc_b': jax.random.normal(k5, (EMBED_DIM,), dtype=jnp.float32) * 0.02}
    _L0_attn_b_in = _L0_attn_b_setup()

    def _L0_ffn_setup():
        import jax, jax.numpy as jnp
        import numpy as np
        B, L, D = (2, 128, 128)
        HID, E, K = (256, 8, 2)
        key = jax.random.key(seed)
        ks = jax.random.split(key, 4)
        std = 0.02
        return {'x': jax.random.normal(ks[0], (B, L, D), dtype=jnp.float32), 'router_scale': jnp.ones((D,), dtype=jnp.float32), 'router_w': jax.random.normal(ks[1], (D, E), dtype=jnp.float32) * std, 'gating_w': jax.random.normal(ks[2], (E, 2, HID, D), dtype=jnp.float32) * std, 'linear_w': jax.random.normal(ks[3], (E, HID, D), dtype=jnp.float32) * std, 'per_expert_scale': jnp.ones((E,), dtype=jnp.float32)}
    _L0_ffn_in = _L0_ffn_setup()
    _d = {'L0_attn_a_x': _L0_attn_a_in['x'], 'L0_attn_a_Wq': _L0_attn_a_in['Wq'], 'L0_attn_a_bq': _L0_attn_a_in['bq'], 'L0_attn_a_Wk': _L0_attn_a_in['Wk'], 'L0_attn_a_bk': _L0_attn_a_in['bk'], 'L0_attn_a_Wv': _L0_attn_a_in['Wv'], 'L0_attn_a_bv': _L0_attn_a_in['bv'], 'L0_attn_a_Wo': _L0_attn_a_in['Wo'], 'L0_attn_a_bo': _L0_attn_a_in['bo'], 'L0_attn_b_head_mask': _L0_attn_b_in['head_mask'], 'L0_attn_b_qkv_w': _L0_attn_b_in['qkv_w'], 'L0_attn_b_qkv_b': _L0_attn_b_in['qkv_b'], 'L0_attn_b_fc_w': _L0_attn_b_in['fc_w'], 'L0_attn_b_fc_b': _L0_attn_b_in['fc_b'], 'L0_ffn_router_scale': _L0_ffn_in['router_scale'], 'L0_ffn_router_w': _L0_ffn_in['router_w'], 'L0_ffn_gating_w': _L0_ffn_in['gating_w'], 'L0_ffn_linear_w': _L0_ffn_in['linear_w'], 'L0_ffn_per_expert_scale': _L0_ffn_in['per_expert_scale']}
    _x0 = _d['L0_attn_a_x']
    _d['L0_attn_a_x'] = jax.random.normal(jax.random.fold_in(jax.random.key(seed), 1), (8, 512, 128), dtype=_x0.dtype)
    del _x0
    return _d

def reference(L0_attn_a_x, L0_attn_a_Wq, L0_attn_a_bq, L0_attn_a_Wk, L0_attn_a_bk, L0_attn_a_Wv, L0_attn_a_bv, L0_attn_a_Wo, L0_attn_a_bo, L0_attn_b_head_mask, L0_attn_b_qkv_w, L0_attn_b_qkv_b, L0_attn_b_fc_w, L0_attn_b_fc_b, L0_ffn_router_scale, L0_ffn_router_w, L0_ffn_gating_w, L0_ffn_linear_w, L0_ffn_per_expert_scale):

    def _L0_attn_a_ref(x, Wq, bq, Wk, bk, Wv, bv, Wo, bo):
        import jax, jax.numpy as jnp
        import numpy as np
        B, S, E = (4, 512, 128)
        CHUNK = 32
        b, s, e = x.shape
        nc = s // CHUNK
        scale = 1.0 / jnp.sqrt(jnp.asarray(e, x.dtype))
        Q = (x @ Wq + bq).reshape(b, nc, CHUNK, e)
        K = (x @ Wk + bk).reshape(b, nc, CHUNK, e)
        V = (x @ Wv + bv).reshape(b, nc, CHUNK, e)
        local_scores = jnp.einsum('bnqe,bnke->bnqk', Q, K) * scale
        local = jnp.einsum('bnqk,bnke->bnqe', jax.nn.softmax(local_scores, axis=-1), V)
        cross_scores = jnp.einsum('bnqe,bmke->bnmqk', Q, K) * scale
        cross = jnp.einsum('bnmqk,bnke->bnqe', jax.nn.softmax(cross_scores, axis=-1), V)
        combined = (local + cross).reshape(b, s, e)
        return combined @ Wo + bo

    def _L0_attn_b_ref(x, head_mask, qkv_w, qkv_b, fc_w, fc_b):
        import jax, jax.numpy as jnp
        import numpy as np
        EMBED_DIM = 128
        NUM_HEADS = 16
        HEAD_DIM = EMBED_DIM // NUM_HEADS
        BATCH = 2
        SEQ = 256
        N, S, D = x.shape
        H, hd = (NUM_HEADS, HEAD_DIM)
        qkv = jnp.einsum('nsd,ed->nse', x, qkv_w) + qkv_b
        qkv = qkv.reshape(N, S, H, 3, hd).transpose(3, 0, 2, 1, 4)
        q, k, v = (qkv[0], qkv[1], qkv[2])
        hm = head_mask.reshape(1, H, 1, 1)
        q = q * hm
        k = k * hm
        v = v * hm
        energy = jnp.einsum('nhqd,nhkd->nhqk', q, k)
        attention = jax.nn.softmax(energy / jnp.sqrt(jnp.float32(hd)), axis=-1)
        out = jnp.einsum('nhqk,nhkd->nhqd', attention, v)
        out = out.transpose(0, 2, 1, 3).reshape(N, S, H * hd)
        out = jnp.einsum('nsd,ed->nse', out, fc_w) + fc_b
        return out

    def _L0_ffn_ref(x, router_scale, router_w, gating_w, linear_w, per_expert_scale):
        import jax, jax.numpy as jnp
        import numpy as np
        B, L, D = (2, 128, 128)
        HID, E, K = (256, 8, 2)
        d = x.shape[-1]
        var = jnp.mean(jnp.square(x), axis=-1, keepdims=True)
        r_in = x * jax.lax.rsqrt(var + 1e-06)
        r_in = r_in * jax.lax.rsqrt(jnp.array(d, dtype=r_in.dtype)) * router_scale
        logits = jnp.dot(r_in, router_w).astype(jnp.float32)
        probs = jax.nn.softmax(logits, axis=-1)
        _, top_k_idx = jax.lax.top_k(logits, K)
        indicator = jax.nn.one_hot(top_k_idx, probs.shape[-1], dtype=probs.dtype)
        gate_weights = indicator.sum(axis=-2) * probs
        renorm = jnp.sum(gate_weights, axis=-1, keepdims=True)
        renorm = jnp.where(renorm > 0.0, renorm, 1.0)
        weights = probs / renorm
        top_k_w = jnp.take_along_axis(weights, top_k_idx, axis=-1)
        combine = jnp.einsum('blke,blk->ble', indicator, top_k_w)
        combine = combine * per_expert_scale
        gate0 = jnp.einsum('bld,ehd->bleh', x, gating_w[:, 0])
        gate1 = jnp.einsum('bld,ehd->bleh', x, gating_w[:, 1])
        act = jax.nn.gelu(gate0) * gate1
        out = jnp.einsum('bleh,ehd,ble->bld', act, linear_w, combine)
        return out.astype(x.dtype)
    x = L0_attn_a_x
    x = x + _L0_attn_a_ref(_layernorm(x, axis=-1), L0_attn_a_Wq, L0_attn_a_bq, L0_attn_a_Wk, L0_attn_a_bk, L0_attn_a_Wv, L0_attn_a_bv, L0_attn_a_Wo, L0_attn_a_bo)
    x = x + _L0_ffn_ref(_layernorm(x, axis=-1), L0_ffn_router_scale, L0_ffn_router_w, L0_ffn_gating_w, L0_ffn_linear_w, L0_ffn_per_expert_scale)
    x = x + _L0_attn_b_ref(_layernorm(x, axis=-1), L0_attn_b_head_mask, L0_attn_b_qkv_w, L0_attn_b_qkv_b, L0_attn_b_fc_w, L0_attn_b_fc_b)
    x = x + _L0_ffn_ref(_layernorm(x, axis=-1), L0_ffn_router_scale, L0_ffn_router_w, L0_ffn_gating_w, L0_ffn_linear_w, L0_ffn_per_expert_scale)
    return x

_drawn_inputs = setup_inputs


def setup_inputs(seed=0):
    import zlib

    import numpy as np

    out = dict(_drawn_inputs(seed))
    spreads = {'L0_ffn_router_scale': (1.0, 0.6), 'L0_ffn_per_expert_scale': (1.0, 0.6)}
    factors = {'L0_attn_a_bq': 8.0,
     'L0_attn_a_bk': 8.0,
     'L0_attn_a_bo': 8.0,
     'L0_attn_b_qkv_b': 8.0,
     'L0_attn_b_fc_b': 8.0,
     'L0_ffn_router_w': 8.0,
     'L0_ffn_gating_w': 8.0,
     'L0_ffn_linear_w': 8.0}
    for name, (base, spread) in spreads.items():
        noise = np.random.default_rng([zlib.crc32(name.encode()), seed]).standard_normal(out[name].shape)
        drawn = base * np.exp(spread * noise) if base else spread * noise
        out[name] = jnp.asarray(drawn.astype(out[name].dtype))
    for name, factor in factors.items():
        out[name] = (out[name] * factor).astype(out[name].dtype)
    return out
```

```python
import concourse.bass as bass
from concourse import mybir
from concourse.alu_op_type import AluOpType as ALU
from contextlib import ExitStack

ACT = mybir.ActivationFunctionType
AX = mybir.AxisListType
F32 = mybir.dt.float32
F32R = mybir.dt.float32r
U32 = mybir.dt.uint32

P = 128
B = 8
T = 4
S = P * T
CHUNK = 32
NC = S // CHUNK
H, HD = 16, 8
G = 4
GH = H // G
NE, HID = 8, 256
UNITS = NE * HID // P
ONE = 24
SCALE_A = float(P) ** -0.5
SCALE_B = float(HD) ** -0.5
AHEAD = 3
ACTS = 4
EBUFS = 4
PLACED = {8: ((0, 0),), 9: ((0, 1),), 10: ((1, 0), (1, 1)), 12: ((2, 0),), 14: ((2, 1),)}
N_CONST = 18

ROUTE_LINKS = 15
STEPS = G * T
LEAD = T + 1


def build(nc, d, out, stages=4):
    with ExitStack() as ctx:
        def sb(name, shape, dt=F32):
            return ctx.enter_context(nc.sbuf_tensor(name, shape, dt))

        def sem(name):
            return ctx.enter_context(nc.semaphore(name))

        banks = ctx.enter_context(nc.psum_tensor("banks", [P, 8, S], F32))
        bank = [banks[:, n, :] for n in range(8)]
        KEY_BANKS = (2, 4)

        res = sb("res", [P, B * T, P])
        xcols = sb("xcols", [P, B * S])
        xh, xl = sb("xh", [P, 2, S], F32R), sb("xl", [P, 2, S], F32R)
        combt = sb("combt", [2 * NE, S], F32R)
        combc = sb("combc", [P, T, 2 * NE])
        comb16 = sb("comb16", [P, B * T, 2 * NE])

        wq, wk, wv, wo = (sb(n, [P, P]) for n in ("wq", "wk", "wv", "wo"))
        wqb, wkb, wvb, wfc = (sb(n, [P, P]) for n in ("wqb", "wkb", "wvb", "wfc"))
        cols = sb("cols", [P, 10])
        rows = sb("rows", [P, 5, P])
        rw, rws = sb("rw", [P, NE]), sb("rws", [P, NE])
        pes = sb("pes", [P, NE])
        ident = sb("ident", [P, P])
        identr = sb("identr", [P, P], F32R)
        own = sb("own", [P, T, NC])
        block_mask = sb("block_mask", [P, T, CHUNK])
        iota = sb("iota", [P, NE])
        placer = sb("placer", [P, 4, G, P], F32R)
        pick = sb("pick", [2 * NE, NE])
        pickr = sb("pickr", [2 * NE, NE], F32R)
        wstage = sb("wstage", [P, 3 * UNITS * P])
        wh, wl = sb("wh", [P, 3 * UNITS * P], F32R), sb("wl", [P, 3 * UNITS * P], F32R)

        stat = sb("stat", [P, T, 6])
        mv = sb("mv", [P, T, 2])
        rstd = sb("rstd", [P, T])
        xn = sb("xn", [P, T, P])
        xt = sb("xt", [P, S])
        rs = sb("rs", [P, T])
        consts = sb("consts", [P, 3, T])
        lg, lgn, ex8, sel, sel2, comb = (sb(n, [P, T, NE]) for n in ("lg", "lgn", "ex8", "sel", "sel2", "comb"))
        top = sb("top", [P, T, NE])
        topi = sb("topi", [P, T, NE], U32)
        topf = sb("topf", [P, T, 2])
        tot, ren, low0, rec1 = (sb(n, [P, T]) for n in ("tot", "ren", "low0", "rec1"))
        combh = sb("combh", [P, T, NE], F32R)

        qt, kt = sb("qt", [P, S]), sb("kt", [P, S])
        v = sb("v", [P, T, P])
        nmax = sb("nmax", [P, T, NC])
        tsum = sb("tsum", [P, T, NC])
        wgt = sb("wgt", [P, T, NC])
        shifted = sb("shifted", [P, T, S])
        expd = sb("expd", [P, T, S])
        place = expd[:, :, :].rearrange("p a (g q) -> p a g q", g=G)
        attn = sb("attn", [P, T, CHUNK])
        abd = sb("abd", [P, T, P])
        tcol = sb("tcol", [P, S])
        ccol = sb("ccol", [P, S])

        qv, kv = qt, kt
        qh, ql = sb("qh", [P, S], F32R), sb("ql", [P, S], F32R)
        pair = sb("pair", [P, 3 * G, S], F32R)
        qp = pair[:, 0:G, :]
        kp = pair[:, G:3 * G, :].rearrange("p (a g) s -> p a g s", a=2)
        qpm = sb("qpm", [P, 2, S], F32R)
        kh, kl = sb("kh", [P, S], F32R), sb("kl", [P, S], F32R)
        nm = sb("nm", [P, 2, T, GH])
        mpad = sb("mpad", [P, T, GH, 32], F32R)
        va = wstage[:, 2 * UNITS * P:].rearrange("p (t h c) -> p t h c", t=T, h=H)
        eb = wstage[:, 0:2 * UNITS * P].rearrange("p (n s) -> p n s", s=2 * S)
        rden = sb("rden", [P, T, GH])
        on = abd
        ov = tcol

        gel, prod = expd[:, 0:2, :], expd[:, 2:4, :]
        act = shifted
        acth, actl = pair[:, 0:ACTS, :], pair[:, ACTS:2 * ACTS, :]
        ocol = ccol

        names = """x_loaded w_loaded ffw_loaded consts_ready passed stat_in stat_ff mv_in mv_ff var_in var_ff rstd_in rstd_ff top_ready pool_link half_ready rs_ready rws_ready wh_ready wl_ready
            link a_link norm_link mpad_link lg_ready vb_ready normed xt_ps xt_ready bias_added
            q_ps qt_ready v_ready s_ps shift_done exp_done wgt_ready weighted attn_ready abd_ready abd_ps
            abdt_ready c_ps ct_ready o_ps res_a
            normed2 xt2_ps xt2_ready xcols_ready xh_ready xl_ready logit_ps lgn_ready ex8_ready comb_ready comb_ps combt_ready
            combc_ready gates gel_done prod_done cb_ps act_done acth_done actl_done down ocol_ready ot_ps res_f
            bnormed bxt_ps bxt_ready bqkv_ps qv_ready qh_ready ql_ready va_ready kp_ps kp_ready qp_ps qp_ready
            sc_ps sc_max mpad_ready qpm_ps qpm_ready st_ps st_exp pv_done ov_ready on_ps on_ready ont_ps
            ont_ready fc_ps res_b stored zeroed""".split()
        m = {n: sem(n) for n in names}

        block = ctx.enter_context(nc.Block())

        def tile(i, t):
            return res[:, bass.ds(i * T + t, 1), :].rearrange("p a d -> p (a d)")

        def batch(i):
            return res[:, bass.ds(i * T, T), :]

        def at_first(i):
            return isinstance(i, int) and i == 0

        def over_batches(engine, first, body):
            body(first, 0, 0, False, True)
            with engine.Fori(0, (B - 2) // 2) as j:
                for k in range(2):
                    i = j * 2 + 1 + k
                    body(i + first, i, 1 - k, True, True)
            body(first + B - 1, B - 1, 1, True, False)

        def over_tiles(ap2):
            return ap2.unsqueeze(1).to_broadcast([P, T, P])

        @block.sync
        def _(sp):
            x_rows = d["x"].rearrange("(b t p) e -> b p t e", t=T, p=P)
            sp.dma_start(batch(0), x_rows[0]).then_inc(m["x_loaded"], 16)
            with sp.Fori(1, B) as i:
                sp.wait_ge(m["x_loaded"], i * 16)
                sp.dma_start(batch(i), x_rows[bass.ds(i, 1)].rearrange("b p t e -> p (b t) e")).then_inc(m["x_loaded"], 16)
            o_rows = out.rearrange("(b t p) e -> b p t e", t=T, p=P)
            n_res = {1: "res_a", 2: "res_f", 3: "res_b", 4: "res_f"}[stages]
            with sp.Fori(0, B) as i:
                sp.wait_ge(m[n_res], i + 1 + (B if stages == 4 else 0))
                sp.dma_start(o_rows[bass.ds(i, 1)].rearrange("b p t e -> p (b t) e"), batch(i)).then_inc(m["stored"], 16)
            sp.wait_ge(m["stored"], 16 * B)

        @block.vector
        def _(dve):
            link_at = [0]

            def chain(i, per, base):
                k = [0]

                def link(ins, alone=False):
                    ins.then_inc(m["link"], 1)
                    k[0] += 1
                    dve.wait_ge(m["link"], i * per + base + k[0])
                    if alone:
                        dve.sem_inc(m["passed"], 1)
                return link, k

            def statistics(i, n, kind):
                dve.sem_inc(m["passed"], 1)
                for t in range(T):
                    last = dve.bn_stats(stat[:, t, :], tile(i, t))
                last.then_inc(m["stat_" + kind], 1)
                dve.wait_ge(m["stat_" + kind], n + 1)
                dve.sem_inc(m["passed"], 1)
                for t in range(T):
                    last = dve.bn_aggr(mv[:, t, :], stat[:, t, :])
                last.then_inc(m["mv_" + kind], 1)

            def normalised(i, n, kind, done):
                dve.wait_ge(m["rstd_" + kind], n + 1)
                for t in range(T):
                    last = dve.tensor_scalar(xn[:, t, :], tile(i, t), mv[:, t, 0:1], rstd[:, t:t + 1],
                                             ALU.subtract, ALU.mult)
                last.then_inc(m[done], 1)

            def chain(n):
                k = [0]

                def link(ins, alone=False):
                    ins.then_inc(m["link"], 1)
                    k[0] += 1
                    dve.wait_ge(m["link"], n * ROUTE_LINKS + k[0])
                    if alone:
                        dve.sem_inc(m["passed"], 1)
                return link, k

            def route_logits(n, products):
                dve.wait_ge(m["rs_ready"], n + 1)
                dve.wait_ge(m["logit_ps"], n + 1)
                dve.tensor_tensor(lg[:, :, :], products[:, 0:T * NE].rearrange("p (t e) -> p t e", e=NE),
                                  rs[:, :].unsqueeze(2).to_broadcast([P, T, NE]), ALU.mult).then_inc(m["lg_ready"], 1)
                dve.wait_ge(m["lg_ready"], n + 1)
                dve.sem_inc(m["passed"], 1)
                for t in range(T):
                    last = dve.max(top[:, t, :], lg[:, t, :])
                last.then_inc(m["top_ready"], 1)
                dve.wait_ge(m["top_ready"], n + 1)
                dve.tensor_tensor(lgn[:, :, :], lg[:, :, :], top[:, :, 0:1].to_broadcast([P, T, NE]),
                                  ALU.subtract).then_inc(m["lgn_ready"], 1)

            def route_weights(i, n):
                link, k = chain(n)
                for t in range(T):
                    last = dve.max_index(topi[:, t, :], top[:, t, :], lg[:, t, :])
                link(last)
                link(dve.tensor_copy(topf[:, :, :], topi[:, :, 0:2]))
                iota_t = iota[:, :].unsqueeze(1).to_broadcast([P, T, NE])
                dve.tensor_tensor(sel[:, :, :], iota_t, topf[:, :, 0:1].to_broadcast([P, T, NE]), ALU.is_equal)
                link(dve.tensor_tensor(sel2[:, :, :], iota_t, topf[:, :, 1:2].to_broadcast([P, T, NE]), ALU.is_equal))
                link(dve.tensor_tensor(sel[:, :, :], sel[:, :, :], sel2[:, :, :], ALU.add))
                dve.wait_ge(m["ex8_ready"], n + 1)
                link(dve.tensor_reduce(tot[:, :], ex8[:, :, :], AX.X, ALU.add))
                link(dve.reciprocal(rec1[:, :], tot[:, :]))
                link(dve.tensor_tensor(comb[:, :, :], ex8[:, :, :], rec1[:, :].unsqueeze(2).to_broadcast([P, T, NE]), ALU.mult))
                link(dve.tensor_tensor(comb[:, :, :], comb[:, :, :], sel[:, :, :], ALU.mult))
                link(dve.tensor_reduce(ren[:, :], comb[:, :, :], AX.X, ALU.add))
                link(dve.tensor_scalar(low0[:, :], ren[:, :], 0.0, None, ALU.is_le))
                link(dve.tensor_tensor(ren[:, :], ren[:, :], low0[:, :], ALU.max))
                link(dve.reciprocal(rec1[:, :], ren[:, :]))
                link(dve.tensor_tensor(comb[:, :, :], comb[:, :, :], rec1[:, :].unsqueeze(2).to_broadcast([P, T, NE]), ALU.mult))
                link(dve.tensor_tensor(comb[:, :, :], comb[:, :, :], pes[:, :].unsqueeze(1).to_broadcast([P, T, NE]), ALU.mult))
                link(dve.tensor_copy(combh[:, :, :], comb[:, :, :]))
                dve.tensor_copy(comb16[:, bass.ds(i * T, T), 0:NE], combh[:, :, :])
                dve.tensor_tensor(comb16[:, bass.ds(i * T, T), NE:2 * NE], comb[:, :, :], combh[:, :, :], ALU.subtract).then_inc(m["comb_ready"], 1)
                assert k[0] == ROUTE_LINKS, k[0]

            dve.wait_ge(m["w_loaded"], 16 * N_CONST)
            dve.tensor_copy(identr[:, :], ident[:, :])
            dve.tensor_copy(placer[:, :, :, :], place[:, :, :, :])
            dve.tensor_copy(pickr[:, :], pick[:, :])
            dve.memset(mpad[:, :, :, :].rearrange("p t h c -> p (t h c)").bitcast(F32), 0.0).then_inc(m["consts_ready"], 1)
            dve.tensor_scalar(rws[:, :], rw[:, :], cols[:, 5:6], SCALE_A, ALU.mult, ALU.mult).then_inc(m["rws_ready"], 1)

            with dve.Fori(0, B) as i:
                k = [0]

                def link(ins):
                    ins.then_inc(m["a_link"], 1)
                    k[0] += 1
                    dve.wait_ge(m["a_link"], i * 3 * T + k[0])

                dve.wait_ge(m["x_loaded"], i * 16 + 16)
                statistics(i, i, "in")
                normalised(i, i, "in", "normed")
                dve.wait_ge(m["q_ps"], i * 3 + 3)
                dve.tensor_tensor(v[:, :, :], bank[3][:, :].rearrange("p (t e) -> p t e", e=P), over_tiles(rows[:, 0, :]),
                                  ALU.add).then_inc(m["v_ready"], 1)

                def shift(t):
                    dve.wait_ge(m["s_ps"], i * T + t + 1)
                    scores = bank[4 + t][:, :].rearrange("p (m k) -> p m k", k=CHUNK)
                    link(dve.tensor_reduce(nmax[:, t, :], scores, AX.X, ALU.max, negate=True))
                    dve.tensor_tensor(shifted[:, t, :].rearrange("p (m k) -> p m k", k=CHUNK), scores,
                                      nmax[:, t, :].unsqueeze(2).to_broadcast([P, NC, CHUNK]), ALU.add).then_inc(m["shift_done"], 1)

                def weigh(t):
                    dve.wait_ge(m["exp_done"], i * T + t + 1)
                    link(dve.tensor_reduce(tsum[:, t, :], expd[:, t, :].rearrange("p (m k) -> p m k", k=CHUNK), AX.X, ALU.add))
                    link(dve.reciprocal(tsum[:, t, :], tsum[:, t, :]))
                    dve.tensor_tensor(wgt[:, t, :], tsum[:, t, :], own[:, t, :], ALU.mult).then_inc(m["wgt_ready"], 1)

                def collect(t):
                    dve.wait_ge(m["weighted"], i * T + t + 1)
                    dve.tensor_reduce(attn[:, t, :], shifted[:, t, :].rearrange("p (m k) -> p k m", k=CHUNK), AX.X,
                                      ALU.add).then_inc(m["attn_ready"], 1)

                for step, t in ((shift, 0), (shift, 1), (weigh, 0), (shift, 2), (weigh, 1), (collect, 0), (shift, 3),
                                (weigh, 2), (collect, 1), (weigh, 3), (collect, 2), (collect, 3)):
                    step(t)
                dve.wait_ge(m["o_ps"], i + 1)
                dve.wait_ge(m["bias_added"], i + 1)
                dve.tensor_tensor(batch(i), batch(i), bank[2][:, :].rearrange("p (t e) -> p t e", e=P),
                                  ALU.add).then_inc(m["res_a"], 1)
                dve.wait_ge(m["res_a"], i + 1)
                statistics(i, i, "ff")
                normalised(i, i, "ff", "normed2")
                route_logits(i, bank[4])
                route_weights(i, i)
                assert k[0] == 3 * T, k[0]

            dve.wait_ge(m["wh_ready"], 1)
            dve.tensor_tensor(wl[:, :], wstage[:, :], wh[:, :], ALU.subtract).then_inc(m["wl_ready"], 1)
            dve.wait_ge(m["wl_ready"], 1)
            dve.memset(wstage[:, 2 * UNITS * P:], 0.0).then_inc(m["zeroed"], 1)
            dve.wait_ge(m["zeroed"], 1)
            dve.memset(va[:, :, :, HD:HD + 1], 1.0)

            def ff_batch(n, i, parity, before, after):
                for u in range(UNITS):
                    dve.wait_ge(m["gel_done"], n * UNITS + u + 1)
                    dve.tensor_tensor(prod[:, u % 2, :], bank[2 + u % 2][:, :], gel[:, u % 2, :], ALU.mult).then_inc(m["prod_done"], 1)
                    if u % 2 == 0:
                        dve.wait_ge(m["cb_ps"], n * NE + u // 2 + 1)
                    dve.wait_ge(m["prod_done"], n * UNITS + u + 1)
                    if u >= ACTS or before:
                        dve.wait_ge(m["actl_done"], n * UNITS + u - ACTS + 1)
                    dve.tensor_tensor(act[:, u % ACTS, :], bank[4 + (u // 2) % 2][:, :], prod[:, u % 2, :], ALU.mult).then_inc(m["act_done"], 1)
                    if u == AHEAD + 2 and before:
                        ff_out(n - 1, i - 1)

            def ff_out(n, i):
                dve.wait_ge(m["ot_ps"], n + 1)
                dve.tensor_tensor(batch(i), batch(i), bank[7][:, :].rearrange("p (t e) -> p t e", e=P),
                                  ALU.add).then_inc(m["res_f"], 1)

            def feed_forward(first):
                over_batches(dve, first, ff_batch)
                ff_out(first + B - 1, B - 1)
            if stages >= 2:
                feed_forward(0)
            def maxima(i, at):
                for hh in range(GH):
                    n = i * (H * T) + at * GH + hh
                    dve.wait_ge(m["sc_ps"], n + 1)
                    dve.tensor_reduce(nm[:, at // T % 2, at % T, hh:hh + 1], bank[hh % 2][:, :], AX.X, ALU.max, negate=True).then_inc(m["sc_max"], 1)

            def maxima_rows(b, g):
                dve.wait_ge(m["sc_max"], b * (H * T) + (g + 1) * T * GH)
                if not (at_first(b) and g == 0):
                    dve.wait_ge(m["qpm_ps"], b * G + g)
                    dve.wait_ge(m["mpad_ready"], b * G + g)
                dve.tensor_copy(mpad[:, :, :, ONE], nm[:, g % 2, :, :]).then_inc(m["mpad_link"], 1)
                dve.wait_ge(m["mpad_link"], b * G + g + 1)
                dve.tensor_tensor(mpad[:, :, :, ONE + 1], nm[:, g % 2, :, :], mpad[:, :, :, ONE], ALU.subtract).then_inc(m["mpad_ready"], 1)

            def normalise(b, g):
                dve.wait_ge(m["on_ps"], b * G + g + 1)
                sums = bank[7][:, :].rearrange("p (t h c) -> p t h c", h=GH, c=32)
                dve.reciprocal(rden[:, :, :], sums[:, :, :, HD]).then_inc(m["norm_link"], 1)
                dve.wait_ge(m["norm_link"], b * G + g + 1)
                for t in range(T):
                    last = dve.tensor_tensor(on[:, t, g * 32:g * 32 + 32].rearrange("p (h j) -> p h j", j=HD), sums[:, t, :, 0:HD],
                                             rden[:, t, :].unsqueeze(2).to_broadcast([P, GH, HD]), ALU.mult)
                last.then_inc(m["on_ready"], 1)

            def head_rows(b, n, bias):
                dve.wait_ge(m["bqkv_ps"], b * 3 + n + 1)
                dve.tensor_scalar((qv, kv)[n][:, :], bank[7][:, :], cols[:, bias:bias + 1], cols[:, 4:5], ALU.add, ALU.mult).then_inc(m["qv_ready"], 1)

            def values_in(b):
                dve.wait_ge(m["bqkv_ps"], b * 3 + 3)
                dve.tensor_tensor(v[:, :, :], bank[7][:, :].rearrange("p (t e) -> p t e", e=P), over_tiles(rows[:, 2, :]), ALU.add).then_inc(m["vb_ready"], 1)

            def values_placed(b, g, first=False):
                dve.wait_ge(m["vb_ready"], b + 1)
                if not first:
                    dve.wait_ge(m["pv_done"], b * (G * T) - (G - 1 - g) * T)
                heads = slice(g * GH, (g + 1) * GH)
                dve.tensor_tensor(va[:, :, heads, 0:HD], v[:, :, g * 32:g * 32 + 32].rearrange("p t (h j) -> p t h j", j=HD),
                                  rows[:, 4, g * 32:g * 32 + 32].rearrange("p (h j) -> p h j", j=HD).unsqueeze(1).to_broadcast([P, T, GH, HD]),
                                  ALU.mult).then_inc(m["va_ready"], 1)

            def heads_out(b):
                dve.wait_ge(m["fc_ps"], b + 1)
                dve.wait_ge(m["bias_added"], B + b + 1)
                dve.tensor_tensor(batch(b), batch(b), bank[7][:, :].rearrange("p (t e) -> p t e", e=P), ALU.add).then_inc(m["res_b"], 1)

            def finish_step(b, s, prepared=False):
                if s == 1:
                    normalise(b, G - 1)
                if s == 3:
                    heads_out(b)
                if s == 4:
                    dve.wait_ge(m["res_b"], b + 1)
                    statistics(b, b + B, "ff")
                if s == 5:
                    if prepared:
                        dve.wait_ge(m["bxt_ps"], b + 3)
                    normalised(b, b + B, "ff", "normed2")
                if s == 8:
                    route_logits(b + B, bank[7])
                if s == 10:
                    route_weights(b, b + B)

            def prepare_step(b, s):
                if s == 2:
                    statistics(b, b + B, "in")
                if s == 3:
                    normalised(b, b + B, "in", "bnormed")
                if s == 5:
                    head_rows(b, 0, 2)
                if s == 6:
                    head_rows(b, 1, 3)
                    values_in(b)

            def heads_batch(i, finish, prepare):
                for s in range(STEPS):
                    if s + LEAD < STEPS or prepare:
                        maxima(i, s + LEAD)
                    if s in (5, 9, 13):
                        normalise(i, s // T - 1)
                    if finish:
                        finish_step(i - 1, s, prepare)
                    if prepare:
                        prepare_step(i + 1, s)
                    if s in (2, 6, 10) or (s == 14 and prepare):
                        if s == 14:
                            maxima_rows(i + 1, 0)
                        else:
                            maxima_rows(i, s // T + 1)
                    if s == 1 and finish:
                        values_placed(i, G - 1)
                    if prepare and s in (7, 10, 14):
                        values_placed(i + 1, (7, 10, 14).index(s))

            if stages >= 3:
                for s in (2, 3, 5, 6):
                    prepare_step(0, s)
                for g in range(G):
                    values_placed(0, g, first=True)
                for k in range(LEAD):
                    maxima(0, k)
                    if k == T - 1:
                        maxima_rows(0, 0)
                heads_batch(0, False, True)
                with dve.Fori(1, B - 1) as i:
                    heads_batch(i, True, True)
                heads_batch(B - 1, True, False)
                for s in (1, 3, 4, 5, 8, 10):
                    finish_step(B - 1, s)
            if stages >= 4:
                feed_forward(B)

        @block.scalar
        def _(act_e):
            small = [(wq, "wq"), (wk, "wk"), (wv, "wv"), (wo, "wo"), (wqb, "wqb"), (wkb, "wkb"), (wvb, "wvb"), (wfc, "wfc"),
                     (cols, "cols"), (rw, "rw"), (ident, "ident")]
            for dst, name in small:
                act_e.dma_start(dst[:, :], d[name]).then_inc(m["w_loaded"], 16)
            act_e.dma_start(rows[:, :, :], d["rows"].unsqueeze(0).to_broadcast([P, 5, P])).then_inc(m["w_loaded"], 16)
            act_e.dma_start(pes[:, :], d["pes"].unsqueeze(0).to_broadcast([P, NE])).then_inc(m["w_loaded"], 16)
            act_e.dma_start(own[:, :, :], d["own"]).then_inc(m["w_loaded"], 16)
            act_e.dma_start(block_mask[:, :, :], d["block_mask"]).then_inc(m["w_loaded"], 16)
            act_e.dma_start(iota[:, :], d["iota"]).then_inc(m["w_loaded"], 16)
            act_e.dma_start(place[:, :, :, :], d["place"]).then_inc(m["w_loaded"], 16)
            act_e.dma_start(pick[:, :], d["pick"]).then_inc(m["w_loaded"], 16)
            act_e.dma_start(wstage[:, 0:2 * UNITS * P], d["wgate"]).then_inc(m["ffw_loaded"], 16)
            act_e.dma_start(wstage[:, 2 * UNITS * P:], d["wdown"]).then_inc(m["ffw_loaded"], 16)

            def copy(dst, src):
                return act_e.activation(dst, src, ACT.Copy)

            def route(i, n):
                act_e.wait_ge(m["xt2_ps"], n + 1)
                copy(xt[:, :], bank[3][:, :]).then_inc(m["xt2_ready"], 1)
                act_e.wait_ge(m["lgn_ready"], n + 1)
                act_e.activation(ex8[:, :, :], lgn[:, :, :], ACT.Exp).then_inc(m["ex8_ready"], 1)
                act_e.wait_ge(m["xcols_ready"], n + 1)

            act_e.wait_ge(m["w_loaded"], 16 * N_CONST)
            with act_e.Fori(0, B) as i:
                act_e.wait_ge(m["xt_ps"], i + 1)
                copy(xt[:, :], bank[0][:, :]).then_inc(m["xt_ready"], 1)
                act_e.wait_ge(m["q_ps"], i * 3 + 1)
                act_e.activation(qt[:, :], bank[1][:, :], ACT.Identity, bias=cols[:, 0:1]).then_inc(m["qt_ready"], 1)
                act_e.wait_ge(m["q_ps"], i * 3 + 2)
                act_e.activation(kt[:, :], bank[2][:, :], ACT.Identity, bias=cols[:, 1:2]).then_inc(m["qt_ready"], 1)
                for t in range(T):
                    act_e.wait_ge(m["shift_done"], i * T + t + 1)
                    act_e.activation(expd[:, t, :], shifted[:, t, :], ACT.Exp, scale=SCALE_A).then_inc(m["exp_done"], 1)
                act_e.wait_ge(m["abd_ps"], i + 1)
                copy(tcol[:, :], bank[0][:, :]).then_inc(m["abdt_ready"], 1)
                act_e.wait_ge(m["c_ps"], i + 1)
                copy(ccol[:, :], bank[1][:, :]).then_inc(m["ct_ready"], 1)
                route(i, i)
            act_e.wait_ge(m["ffw_loaded"], 32)
            copy(wh[:, :], wstage[:, :]).then_inc(m["wh_ready"], 1)

            def ff_columns(n, i, parity):
                copy(xh[:, parity, :], xcols[:, bass.ds(i * S, S)]).then_inc(m["xh_ready"], 1)

            def ff_weights(n, i):
                act_e.wait_ge(m["comb_ready"], n + 1)
                copy(combc[:, :, :], comb16[:, bass.ds(i * T, T), :]).then_inc(m["combc_ready"], 1)

            def ff_weight_columns(n):
                act_e.wait_ge(m["comb_ps"], n + 1)
                copy(combt[:, :], bank[7][0:2 * NE, :]).then_inc(m["combt_ready"], 1)

            def ff_high(n, u):
                act_e.wait_ge(m["act_done"], n * UNITS + u + 1)
                copy(acth[:, u % ACTS, :], act[:, u % ACTS, :]).then_inc(m["acth_done"], 1)

            def ff_out(n):
                act_e.wait_ge(m["down"], n * UNITS)
                copy(ocol[:, :], bank[6][:, :]).then_inc(m["ocol_ready"], 1)

            def ff_batch(n, i, parity, before, after):
                for u in range(UNITS):
                    if u == AHEAD and before:
                        ff_out(n)
                    act_e.wait_ge(m["gates"], n * UNITS + u + 1)
                    act_e.activation(gel[:, u % 2, :], bank[u % 2][:, :], ACT.Gelu_apprx_tanh).then_inc(m["gel_done"], 1)
                    if u >= 1 or before:
                        if u > ACTS or before:
                            act_e.wait_ge(m["down"], n * UNITS + u - ACTS)
                        ff_high(n, u - 1) if u else ff_high(n - 1, UNITS - 1)
                    if after and u == 8:
                        ff_columns(n + 1, i + 1, 1 - parity)
                    if after and u == 9:
                        ff_weights(n + 1, i + 1)
                if after:
                    act_e.wait_ge(m["cb_ps"], (n + 1) * NE)
                    ff_weight_columns(n + 1)

            def feed_forward(first):
                act_e.wait_ge(m["xcols_ready"], first + B)
                ff_columns(first, 0, 0)
                ff_weights(first, 0)
                ff_weight_columns(first)
                over_batches(act_e, first, ff_batch)
                ff_high(first + B - 1, UNITS - 1)
                ff_out(first + B)
            if stages >= 2:
                feed_forward(0)
            def placed(b, g, part):
                act_e.wait_ge(m["qp_ps"], b * 2 * G + 2 * g + part + 1)
                if part == 0:
                    copy(qp[:, g, :], bank[7][:, :]).then_inc(m["qp_ready"], 1)
                else:
                    for a in range(2):
                        act_e.activation(kp[:, a, g, :], bank[7][:, :], ACT.Identity, bias=cols[:, 8 + a:9 + a],
                                         scale=cols[:, 6 + a:7 + a]).then_inc(m["qp_ready"], 1)

            def exponentials(i, s):
                gs = i * STEPS + s
                for pair in range(2):
                    n = 2 * s + pair
                    act_e.wait_ge(m["st_ps"], gs * 2 + pair + 1)
                    if not (at_first(i) and n < EBUFS):
                        act_e.wait_ge(m["pv_done"], gs + (pair - EBUFS) // 2 + 1)
                    two = KEY_BANKS[pair]
                    act_e.activation(eb[:, n % EBUFS, :], banks[:, two:two + 2, :].rearrange("p a s -> p (a s)"),
                                     ACT.Exp, scale=SCALE_B).then_inc(m["st_exp"], 1)

            def maxima_in(b, g):
                act_e.wait_ge(m["qpm_ps"], b * G + g + 1)
                copy(qpm[:, g % 2, :], bank[7][:, :]).then_inc(m["qpm_ready"], 1)

            def sums_out(b, g):
                act_e.wait_ge(m["pv_done"], b * (G * T) + (g + 1) * T)
                copy(ov[:, :], bank[6][:, :]).then_inc(m["ov_ready"], 1)

            def finish_step(b, s):
                if s == 0:
                    sums_out(b, G - 1)
                if s == 2:
                    act_e.wait_ge(m["ont_ps"], b + 1)
                    copy(ccol[:, :], bank[7][:, :]).then_inc(m["ont_ready"], 1)
                if s == 7:
                    act_e.wait_ge(m["xt2_ps"], b + B + 1)
                    copy(xt[:, :], bank[7][:, :]).then_inc(m["xt2_ready"], 1)
                if s == 9:
                    act_e.wait_ge(m["lgn_ready"], b + B + 1)
                    act_e.activation(ex8[:, :, :], lgn[:, :, :], ACT.Exp).then_inc(m["ex8_ready"], 1)

            def prepare_step(b, s):
                if s == 4:
                    act_e.wait_ge(m["bxt_ps"], b + 1)
                    act_e.wait_ge(m["xcols_ready"], B if at_first(b) else b + B - 2)
                    copy(xt[:, :], bank[7][:, :]).then_inc(m["bxt_ready"], 1)
                if s == 6:
                    act_e.wait_ge(m["qv_ready"], b * 2 + 1)
                    copy(qh[:, :], qv[:, :]).then_inc(m["qh_ready"], 1)
                if s == 7:
                    act_e.wait_ge(m["qv_ready"], b * 2 + 2)
                    copy(kh[:, :], kv[:, :]).then_inc(m["qh_ready"], 1)
                for g, part in PLACED.get(s, ()):
                    placed(b, g, part)

            def heads_batch(i, finish, prepare):
                for s in range(STEPS):
                    exponentials(i, s)
                    if finish:
                        finish_step(i - 1, s)
                        if s == 0:
                            placed(i, G - 1, 0)
                        if s == 1:
                            placed(i, G - 1, 1)
                    if s in (4, 8, 12):
                        sums_out(i, s // T - 1)
                    if prepare:
                        prepare_step(i + 1, s)
                    if s in (3, 7, 11):
                        maxima_in(i, s // T + 1)
                    if s == 15 and prepare:
                        maxima_in(i + 1, 0)

            if stages >= 3:
                for s in (4, 6, 7):
                    prepare_step(0, s)
                for g in range(G):
                    for part in range(2):
                        placed(0, g, part)
                maxima_in(0, 0)
                heads_batch(0, False, True)
                with act_e.Fori(1, B - 1) as i:
                    heads_batch(i, True, True)
                heads_batch(B - 1, True, False)
                for s in (0, 2, 7, 9):
                    finish_step(B - 1, s)
            if stages >= 4:
                feed_forward(B)

        @block.gpsimd
        def _(pool):
            for n, value in enumerate((-0.5, 1e-5, 1e-6)):
                pool.memset(consts[:, n, :], value).then_inc(m["half_ready"], 1)
            pool.wait_ge(m["w_loaded"], 16 * N_CONST)
            pool.wait_ge(m["half_ready"], 3)

            def deviation(n, kind):
                pool.wait_ge(m["mv_" + kind], n + 1)
                pool.tensor_tensor(rstd[:, :], mv[:, :, 1], consts[:, 1, :], ALU.add).then_inc(m["var_" + kind], 1)
                pool.wait_ge(m["var_" + kind], n + 1)
                pool.tensor_tensor(rstd[:, :], rstd[:, :], consts[:, 0, :], ALU.pow).then_inc(m["rstd_" + kind], 1)

            def route_deviation(n):
                deviation(n, "ff")
                pool.wait_ge(m["rstd_ff"], n + 1)
                for k, (in0, in1, op) in enumerate(((rstd[:, :], rstd[:, :], ALU.mult), (rs[:, :], mv[:, :, 1], ALU.mult),
                                                    (rs[:, :], consts[:, 2, :], ALU.add))):
                    pool.tensor_tensor(rs[:, :], in0, in1, op).then_inc(m["pool_link"], 1)
                    pool.wait_ge(m["pool_link"], n * 3 + k + 1)
                pool.tensor_tensor(rs[:, :], rs[:, :], consts[:, 0, :], ALU.pow).then_inc(m["rs_ready"], 1)

            def route(i, n):
                pool.wait_ge(m["xt2_ready"], n + 1)
                pool.tensor_copy(xcols[:, bass.ds(i * S, S)], xt[:, :]).then_inc(m["xcols_ready"], 1)

            with pool.Fori(0, B) as i:
                deviation(i, "in")
                pool.wait_ge(m["normed"], i + 1)
                pool.tensor_tensor(batch(i), batch(i), over_tiles(rows[:, 1, :]), ALU.add).then_inc(m["bias_added"], 1)
                for t in range(T):
                    pool.wait_ge(m["wgt_ready"], i * T + t + 1)
                    pool.tensor_tensor(shifted[:, t, :].rearrange("p (m k) -> p m k", k=CHUNK),
                                       expd[:, t, :].rearrange("p (m k) -> p m k", k=CHUNK),
                                       wgt[:, t, :].unsqueeze(2).to_broadcast([P, NC, CHUNK]), ALU.mult).then_inc(m["weighted"], 1)
                    if t >= 1:
                        pool.wait_ge(m["attn_ready"], i * T + t)
                        pool.tensor_tensor(abd[:, t - 1, :].rearrange("p (c k) -> p c k", k=CHUNK), block_mask[:, :, :],
                                           attn[:, t - 1, :].unsqueeze(1).to_broadcast([P, T, CHUNK]), ALU.mult).then_inc(m["abd_ready"], 1)
                pool.wait_ge(m["attn_ready"], i * T + T)
                pool.tensor_tensor(abd[:, T - 1, :].rearrange("p (c k) -> p c k", k=CHUNK), block_mask[:, :, :],
                                   attn[:, T - 1, :].unsqueeze(1).to_broadcast([P, T, CHUNK]), ALU.mult).then_inc(m["abd_ready"], 1)
                route_deviation(i)
                route(i, i)

            def ff_columns(n, i, parity):
                pool.wait_ge(m["xh_ready"], n + 1)
                pool.tensor_tensor(xl[:, parity, :], xcols[:, bass.ds(i * S, S)], xh[:, parity, :], ALU.subtract).then_inc(m["xl_ready"], 1)

            def ff_batch(n, i, parity, before, after):
                for u in range(UNITS):
                    pool.wait_ge(m["acth_done"], n * UNITS + u + 1)
                    pool.tensor_tensor(actl[:, u % ACTS, :], act[:, u % ACTS, :], acth[:, u % ACTS, :],
                                       ALU.subtract).then_inc(m["actl_done"], 1)
                    if after and u == 8:
                        ff_columns(n + 1, i + 1, 1 - parity)

            def feed_forward(first):
                ff_columns(first, 0, 0)
                over_batches(pool, first, ff_batch)
            if stages >= 2:
                feed_forward(0)
            def prepare(b):
                deviation(b + B, "in")
                pool.wait_ge(m["bnormed"], b + 1)
                pool.tensor_tensor(batch(b), batch(b), over_tiles(rows[:, 3, :]), ALU.add).then_inc(m["bias_added"], 1)

            def split(b):
                pool.wait_ge(m["qh_ready"], b * 2 + 1)
                pool.tensor_tensor(ql[:, :], qv[:, :], qh[:, :], ALU.subtract).then_inc(m["ql_ready"], 1)
                pool.wait_ge(m["qh_ready"], b * 2 + 2)
                pool.tensor_tensor(kl[:, :], kv[:, :], kh[:, :], ALU.subtract).then_inc(m["ql_ready"], 1)

            if stages >= 3:
                prepare(0)
                split(0)
                prepare(1)
                split(1)
                with pool.Fori(1, B - 1) as i:
                    prepare(i + 1)
                    route_deviation(i - 1 + B)
                    split(i + 1)
                    route(i - 1, i - 1 + B)
                for b in (B - 2, B - 1):
                    route_deviation(b + B)
                    route(b, b + B)
            if stages >= 4:
                feed_forward(B)

        @block.tensor
        def _(pe):
            pe.wait_ge(m["w_loaded"], 16 * N_CONST)
            pe.wait_ge(m["consts_ready"], 1)
            pe.wait_ge(m["rws_ready"], 1)

            def transposes(to, src, rows_out=P):
                for t in range(T):
                    last = pe.transpose(to[0:rows_out, t * P:(t + 1) * P], src[:, t, :], ident[:, :])
                return last

            def by_tile(to, columns, w):
                for t in range(T):
                    last = pe.matmul(to[:, t * P:(t + 1) * P], columns[:, t * P:(t + 1) * P], w, start=True, stop=True)
                return last

            def logits(n, to):
                pe.wait_ge(m["xt2_ready"], n + 1)
                for t in range(T):
                    last = pe.matmul(to[:, t * NE:(t + 1) * NE], xt[:, t * P:(t + 1) * P], rws[:, :], start=True, stop=True)
                last.then_inc(m["logit_ps"], 1)

            with pe.Fori(0, B) as i:
                pe.wait_ge(m["normed"], i + 1)
                transposes(bank[0], xn).then_inc(m["xt_ps"], 1)
                pe.wait_ge(m["xt_ready"], i + 1)
                pe.matmul(bank[1][:, :], wq[:, :], xt[:, :], start=True, stop=True).then_inc(m["q_ps"], 1)
                pe.matmul(bank[2][:, :], wk[:, :], xt[:, :], start=True, stop=True).then_inc(m["q_ps"], 1)
                by_tile(bank[3], xt, wv[:, :]).then_inc(m["q_ps"], 1)
                pe.wait_ge(m["qt_ready"], i * 2 + 2)
                for t in range(T):
                    pe.matmul(bank[4 + t][:, :], qt[:, t * P:(t + 1) * P], kt[:, :], start=True, stop=True).then_inc(m["s_ps"], 1)
                for t in range(T):
                    pe.wait_ge(m["abd_ready"], i * T + t + 1)
                    last = pe.transpose(bank[0][:, t * P:(t + 1) * P], abd[:, t, :], ident[:, :])
                last.then_inc(m["abd_ps"], 1)
                pe.wait_ge(m["abdt_ready"], i + 1)
                pe.wait_ge(m["v_ready"], i + 1)
                for t in range(T):
                    last = pe.matmul(bank[1][:, t * P:(t + 1) * P], v[:, t, :], tcol[:, t * P:(t + 1) * P], start=True, stop=True)
                last.then_inc(m["c_ps"], 1)
                pe.wait_ge(m["ct_ready"], i + 1)
                by_tile(bank[2], ccol, wo[:, :]).then_inc(m["o_ps"], 1)
                pe.wait_ge(m["normed2"], i + 1)
                transposes(bank[3], xn).then_inc(m["xt2_ps"], 1)
                logits(i, bank[4])

            def three(to, w0, high, low, start, stop):
                pe.matmul(to, wh[:, w0:w0 + P], high, start=start, stop=False)
                pe.matmul(to, wh[:, w0:w0 + P], low, start=False, stop=False)
                return pe.matmul(to, wl[:, w0:w0 + P], high, start=False, stop=stop)

            def ff_weight_columns(n):
                pe.wait_ge(m["combc_ready"], n + 1)
                transposes(bank[7], combc, 2 * NE).then_inc(m["comb_ps"], 1)

            def ff_down(n, u):
                pe.wait_ge(m["actl_done"], n * UNITS + u + 1)
                three(bank[6][:, :], (2 * UNITS + u) * P, acth[:, u % ACTS, :], actl[:, u % ACTS, :],
                      u == 0, u == UNITS - 1).then_inc(m["down"], 1)

            def ff_out(n):
                pe.wait_ge(m["ocol_ready"], n + 1)
                for t in range(T):
                    last = pe.transpose(bank[7][:, t * P:(t + 1) * P], ocol[:, t * P:(t + 1) * P], ident[:, :])
                last.then_inc(m["ot_ps"], 1)

            def ff_batch(n, i, parity, before, after):
                pe.wait_ge(m["xl_ready"], n + 1)
                for u in range(UNITS):
                    if u >= 2 or before:
                        pe.wait_ge(m["prod_done"], n * UNITS + u - 1)
                    high, low = xh[:, parity, :], xl[:, parity, :]
                    three(bank[u % 2][:, :], u * P, high, low, True, True)
                    three(bank[2 + u % 2][:, :], (UNITS + u) * P, high, low, True, True).then_inc(m["gates"], 1)
                    if u % 2 == 0:
                        if u == 0:
                            pe.wait_ge(m["combt_ready"], n + 1)
                        if u >= 4 or before:
                            pe.wait_ge(m["act_done"], n * UNITS + u - 2)
                        pe.matmul(bank[4 + (u // 2) % 2][:, :], pickr[:, u // 2:u // 2 + 1].to_broadcast([2 * NE, P]), combt[:, :],
                                  start=True, stop=True).then_inc(m["cb_ps"], 1)
                    if u < AHEAD and before:
                        ff_down(n - 1, UNITS + u - AHEAD)
                    if u >= AHEAD:
                        if u == AHEAD and before:
                            pe.wait_ge(m["ocol_ready"], n)
                        ff_down(n, u - AHEAD)
                    if u == AHEAD + 1 and before:
                        ff_out(n - 1)
                    if u == 11 and after:
                        if before:
                            pe.wait_ge(m["res_f"], n)
                        ff_weight_columns(n + 1)

            def feed_forward(first):
                pe.wait_ge(m["wl_ready"], 1)
                pe.wait_ge(m["comb_ready"], first + B)
                ff_weight_columns(first)
                over_batches(pe, first, ff_batch)
                n = first + B - 1
                for u in range(UNITS - AHEAD, UNITS):
                    ff_down(n, u)
                ff_out(n)
                pe.wait_ge(m["res_f"], n + 1)
            if stages >= 2:
                feed_forward(0)
            side = [None]

            def side_free():
                if side[0] is not None:
                    pe.wait_ge(m[side[0][0]], side[0][1])

            def side_used(name, count):
                side[0] = (name, count)

            def place_rows(b, g, part):
                side_free()
                hi, lo = ((qh, ql), (kh, kl))[part]
                pe.wait_ge(m["ql_ready"], b * 2 + part + 1)
                pe.matmul(bank[7][:, :], placer[:, 2 * part, g, :], hi[:, :], start=True, stop=False)
                pe.matmul(bank[7][:, :], placer[:, 2 * part + 1, g, :], lo[:, :], start=False, stop=True).then_inc(m["qp_ps"], 1)
                side_used("qp_ready", b * 3 * G + 3 * g + 2 * part + 1)

            def score(i, at, hh):
                g, t, r = at // T % G, at % T, 64 * (hh // 2)
                n = i * (H * T) + at * GH + hh
                if not (at_first(i) and at * GH + hh < 2):
                    pe.wait_ge(m["sc_max"], n - 1)
                pe.matmul(bank[hh % 2][:, :], qp[r:r + 64, g, t * P:(t + 1) * P], kp[r:r + 64, hh % 2, g, :],
                          start=True, stop=True, tile_position=(r, 0)).then_inc(m["sc_ps"], 1)

            def max_rows(b, g):
                side_free()
                pe.wait_ge(m["mpad_ready"], b * G + g + 1)
                pe.matmul(bank[7][:, :], identr[:, :], qp[:, g, :], start=True, stop=False)
                for t in range(T):
                    last = pe.matmul(bank[7][:, t * P:(t + 1) * P], mpad[:, t, :, :].rearrange("p h c -> p (h c)"), identr[:, :],
                                     start=False, stop=t == T - 1)
                last.then_inc(m["qpm_ps"], 1)
                side_used("qpm_ready", b * G + g + 1)

            def keys(i, s, hh):
                g, t, r, pair = s // T, s % T, 64 * (hh // 2), hh // 2
                if hh % 2 == 0 and not (at_first(i) and s == 0):
                    pe.wait_ge(m["st_exp"], (i * STEPS + s) * 2 + pair - 1)
                last = pe.matmul(bank[KEY_BANKS[pair] + hh % 2][:, :], kp[r:r + 64, hh % 2, g, t * P:(t + 1) * P], qpm[r:r + 64, g % 2, :],
                                 start=True, stop=True, tile_position=(r, 0))
                if hh % 2:
                    last.then_inc(m["st_ps"], 1)

            def values(i, s):
                g, t = s // T % G, s % T
                pe.wait_ge(m["st_exp"], (i * STEPS + s) * 2 + 2)
                if t == 0 and not (at_first(i) and s == 0):
                    pe.wait_ge(m["ov_ready"], i * G + s // T)
                for hh in range(GH):
                    n = 2 * s + hh // 2
                    last = pe.matmul(bank[6][32 * hh:32 * hh + 32, :], va[:, t, g * GH + hh, :],
                                     eb[:, n % EBUFS, (hh % 2) * S:(hh % 2 + 1) * S], start=t == 0, stop=t == T - 1,
                                     tile_position=(0, 32 * hh))
                last.then_inc(m["pv_done"], 1)

            def to_rows(b, g):
                side_free()
                pe.wait_ge(m["ov_ready"], b * G + g + 1)
                for t in range(T):
                    last = pe.transpose(bank[7][:, t * P:(t + 1) * P], ov[:, t * P:(t + 1) * P], ident[:, :])
                last.then_inc(m["on_ps"], 1)
                side_used("on_ready", b * G + g + 1)

            def finish_step(b, s):
                if s == 1:
                    to_rows(b, G - 1)
                if s == 2:
                    side_free()
                    pe.wait_ge(m["on_ready"], b * G + G)
                    transposes(bank[7], on).then_inc(m["ont_ps"], 1)
                    side_used("ont_ready", b + 1)
                if s == 3:
                    side_free()
                    by_tile(bank[7], ccol, wfc[:, :]).then_inc(m["fc_ps"], 1)
                    side_used("res_b", b + 1)
                if s == 7:
                    side_free()
                    pe.wait_ge(m["normed2"], b + B + 1)
                    transposes(bank[7], xn).then_inc(m["xt2_ps"], 1)
                    side_used("xt2_ready", b + B + 1)
                if s == 8:
                    side_free()
                    logits(b + B, bank[7])
                    side_used("lg_ready", b + B + 1)

            def prepare_step(b, s):
                if s == 4:
                    side_free()
                    pe.wait_ge(m["bnormed"], b + 1)
                    transposes(bank[7], xn).then_inc(m["bxt_ps"], 1)
                    side_used("bxt_ready", b + 1)
                if s in (5, 6):
                    side_free()
                    pe.wait_ge(m["bxt_ready"], b + 1)
                    pe.matmul(bank[7][:, :], (wqb, wkb)[s - 5][:, :], xt[:, :], start=True, stop=True).then_inc(m["bqkv_ps"], 1)
                    side_used("qv_ready", b * 2 + s - 4)
                if s == 6:
                    side_free()
                    by_tile(bank[7], xt, wvb[:, :]).then_inc(m["bqkv_ps"], 1)
                    side_used("vb_ready", b + 1)
                for g, part in PLACED.get(s, ()):
                    place_rows(b, g, part)

            def heads_batch(i, finish, prepare):
                for s in range(STEPS):
                    ahead = s + LEAD < STEPS or prepare
                    at = s + LEAD
                    if at % T == 0 and ahead:
                        pe.wait_ge(m["qp_ready"], i * 3 * G + 3 * (at // T) + 3)
                    if s % T == 0:
                        pe.wait_ge(m["qpm_ready"], i * G + s // T + 1)
                        pe.wait_ge(m["va_ready"], i * G + s // T + 1)
                    for hh in range(GH):
                        if ahead:
                            score(i, at, hh)
                        keys(i, s, hh)
                        if hh == 1 and (s >= 1 or finish):
                            values(i, s - 1)
                    if finish:
                        finish_step(i - 1, s)
                        if s in (0, 1):
                            place_rows(i, G - 1, s)
                    if s in (5, 9, 13):
                        to_rows(i, s // T - 1)
                    if prepare:
                        prepare_step(i + 1, s)
                    if s in (3, 7, 11):
                        max_rows(i, s // T + 1)
                    if s == 15 and prepare:
                        max_rows(i + 1, 0)

            if stages >= 3:
                for s in (4, 5, 6):
                    prepare_step(0, s)
                for g in range(G):
                    for part in range(2):
                        place_rows(0, g, part)
                pe.wait_ge(m["qp_ready"], 3 * G)
                for k in range(LEAD):
                    for hh in range(GH):
                        score(0, k, hh)
                max_rows(0, 0)
                heads_batch(0, False, True)
                with pe.Fori(1, B - 1) as i:
                    side_used("qpm_ready", i * G + 1)
                    heads_batch(i, True, True)
                side_used("qpm_ready", (B - 1) * G + 1)
                heads_batch(B - 1, True, False)
                values(B - 1, STEPS - 1)
                for s in (1, 2, 3, 7, 8):
                    finish_step(B - 1, s)
            if stages >= 4:
                feed_forward(B)


_INS = ("x", "wq", "wk", "wv", "wo", "wqb", "wkb", "wvb", "wfc", "cols", "rows", "rw", "pes", "wgate", "wdown",
        "ident", "own", "block_mask", "iota", "place", "pick")


def kernel(L0_attn_a_x, L0_attn_a_Wq, L0_attn_a_bq, L0_attn_a_Wk, L0_attn_a_bk, L0_attn_a_Wv, L0_attn_a_bv, L0_attn_a_Wo,
           L0_attn_a_bo, L0_attn_b_head_mask, L0_attn_b_qkv_w, L0_attn_b_qkv_b, L0_attn_b_fc_w, L0_attn_b_fc_b,
           L0_ffn_router_scale, L0_ffn_router_w, L0_ffn_gating_w, L0_ffn_linear_w, L0_ffn_per_expert_scale, stages=4):
    import numpy as np
    import concourse.bacc as bacc
    from concourse.bass_utils import run_bass_kernel_spmd

    A = np.asarray
    qkv = A(L0_attn_b_qkv_w).reshape(H, 3, HD, P)
    qkvb = A(L0_attn_b_qkv_b).reshape(H, 3, HD)
    mask = np.repeat(A(L0_attn_b_head_mask), HD)
    p = np.arange(P)
    own = np.where(np.arange(NC)[None, None, :] == np.arange(T)[None, :, None] * T + p[:, None, None] // CHUNK, 2, 1)
    block_mask = np.broadcast_to(np.arange(T)[None, :, None] == p[:, None, None] // CHUNK, (P, T, CHUNK))
    one_rows = (p % 32 == ONE) | (p % 32 == ONE + 1)
    even = p // 32 % 2 == 0
    place = np.zeros((P, 4, G, P), np.float32)
    for part, copies in enumerate(((0, 1), (2,), (0, 2), (1,))):
        for c in copies:
            for h in range(H):
                for j in range(HD):
                    place[h * HD + j, part, h // GH, h % GH * 32 + c * HD + j] = 1
    pick = np.arange(2 * NE)[:, None] % NE == np.arange(NE)[None, :]
    arrays = {
        "x": A(L0_attn_a_x).reshape(B * S, P), "wq": A(L0_attn_a_Wq), "wk": A(L0_attn_a_Wk), "wv": A(L0_attn_a_Wv), "wo": A(L0_attn_a_Wo),
        "wqb": qkv[:, 0].reshape(P, P).T, "wkb": qkv[:, 1].reshape(P, P).T, "wvb": qkv[:, 2].reshape(P, P).T,
        "wfc": A(L0_attn_b_fc_w).T,
        "cols": np.stack([A(L0_attn_a_bq), A(L0_attn_a_bk), qkvb[:, 0].reshape(P), qkvb[:, 1].reshape(P), mask,
                          A(L0_ffn_router_scale)] + [a.astype(np.float32) for a in (even, ~even, even & one_rows, ~even & one_rows)], 1),
        "rows": np.stack([A(L0_attn_a_bv), A(L0_attn_a_bo), qkvb[:, 2].reshape(P), A(L0_attn_b_fc_b), mask]),
        "rw": A(L0_ffn_router_w), "pes": A(L0_ffn_per_expert_scale),
        "wgate": A(L0_ffn_gating_w).transpose(3, 1, 0, 2).reshape(P, 2 * UNITS * P),
        "wdown": A(L0_ffn_linear_w).reshape(UNITS, P, P).transpose(1, 0, 2).reshape(P, UNITS * P),
        "ident": np.eye(P, dtype=np.float32), "own": own.astype(np.float32), "block_mask": block_mask.astype(np.float32),
        "iota": np.broadcast_to(np.arange(NE, dtype=np.float32), (P, NE)), "place": place, "pick": pick.astype(np.float32),
    }
    nc = bacc.Bacc("TRN2", target_bir_lowering=False, num_devices=1)
    sent, d = {}, {}
    for name in _INS:
        a = np.ascontiguousarray(arrays[name])
        sent[f"in_{name}"] = a
        d[name] = nc.dram_tensor(f"in_{name}", a.shape, mybir.dt.from_np(a.dtype), kind="ExternalInput").ap()
    out = nc.dram_tensor("out", (B * S, P), F32, kind="ExternalOutput").ap()
    build(nc, d, out, stages)
    r = run_bass_kernel_spmd(nc, [sent], core_ids=[0])
    return r.results[0]["out"].reshape(B, S, P)
```

```python
import concourse.bass as bass
from concourse import mybir
from concourse.alu_op_type import AluOpType as ALU
from contextlib import ExitStack

ACT = mybir.ActivationFunctionType
AX = mybir.AxisListType
F32 = mybir.dt.float32
F32R = mybir.dt.float32r
U32 = mybir.dt.uint32

P = 128
B = 8
T = 4
S = P * T
CHUNK = 32
NC = S // CHUNK
H, HD = 16, 8
G = 4
GH = H // G
NE, HID = 8, 256
UNITS = NE * HID // P
ONE = 24
SCALE_A = float(P) ** -0.5
SCALE_B = float(HD) ** -0.5
AHEAD = 3
ACTS = 4
EBUFS = 4
PLACED = {(7, 0): (0, 0), (7, 1): (0, 1), (8, 1): (1, 0), (9, 1): (1, 1), (12, 0): (2, 0), (12, 1): (2, 1)}
LATE = ((0, 0), (0, 1))
KINDS = ("in", "ff")
N_CONST = 18

ROUTE_LINKS = 15
STEPS = G * T
LEAD = T + 2


def build(nc, d, out, stages=4):
    with ExitStack() as ctx:
        def sb(name, shape, dt=F32):
            return ctx.enter_context(nc.sbuf_tensor(name, shape, dt))

        def sem(name):
            return ctx.enter_context(nc.semaphore(name))

        banks = ctx.enter_context(nc.psum_tensor("banks", [P, 8, S], F32))
        bank = [banks[:, n, :] for n in range(8)]
        KEY_BANKS = (2, 4)

        res = sb("res", [P, B * T, P])
        xcols = sb("xcols", [P, B * S])
        combt = sb("combt", [2 * NE, S], F32R)
        combc = sb("combc", [P, T, 2 * NE])
        comb16 = sb("comb16", [P, B * T, 2 * NE])

        wq, wk, wv, wo = (sb(n, [P, P]) for n in ("wq", "wk", "wv", "wo"))
        wqb, wkb, wvb, wfc = (sb(n, [P, P]) for n in ("wqb", "wkb", "wvb", "wfc"))
        cols = sb("cols", [P, 7 + GH])
        rows = sb("rows", [P, 5, P])
        rw, rws = sb("rw", [P, NE]), sb("rws", [P, NE])
        pes = sb("pes", [P, NE])
        ident = sb("ident", [P, P])
        identr = sb("identr", [P, P], F32R)
        own = sb("own", [P, T, NC])
        block_mask = sb("block_mask", [P, T, CHUNK])
        iota = sb("iota", [P, NE])
        placer = sb("placer", [P, 4, G, P], F32R)
        pick = sb("pick", [2 * NE, NE])
        pickr = sb("pickr", [2 * NE, NE], F32R)
        wstage = sb("wstage", [P, 3 * UNITS * P])
        wh, wl = sb("wh", [P, 3 * UNITS * P], F32R), sb("wl", [P, 3 * UNITS * P], F32R)

        stat = {k: sb("stat_" + k, [P, T, 6]) for k in KINDS}
        mv = {k: sb("mv_" + k, [P, T, 2]) for k in KINDS}
        rstd = {k: sb("rstd_" + k, [P, T]) for k in KINDS}
        xn = {k: sb("xn_" + k, [P, T, P]) for k in KINDS}
        xt = {k: sb("xt_" + k, [P, S]) for k in KINDS}
        rs = sb("rs", [P, T])
        consts = sb("consts", [P, 3, T])
        lg, lgn, ex8, sel, sel2, comb = (sb(n, [P, T, NE]) for n in ("lg", "lgn", "ex8", "sel", "sel2", "comb"))
        top = sb("top", [P, T, NE])
        topi = sb("topi", [P, T, NE], U32)
        topf = sb("topf", [P, T, 2])
        tot, ren, low0, rec1 = (sb(n, [P, T]) for n in ("tot", "ren", "low0", "rec1"))
        combh = sb("combh", [P, T, NE], F32R)

        qt, kt = sb("qt", [P, S]), sb("kt", [P, S])
        v = sb("v", [P, T, P])
        nmax = sb("nmax", [P, T, NC])
        tsum = sb("tsum", [P, T, NC])
        wgt = sb("wgt", [P, T, NC])
        with nc.sbuf_tensor("shifted", [P, T, S], F32) as shifted, nc.sbuf_tensor("expd", [P, T, S], F32) as expd:
            pass
        room = sb("room", [P, 5 * T, S], F32R)
        place = expd[:, :, :].rearrange("p a (g q) -> p a g q", g=G)
        attn = sb("attn", [P, T, CHUNK])
        abd = sb("abd", [P, T, P])
        tcol = sb("tcol", [P, S])
        ccol = sb("ccol", [P, S])

        qv, kv = qt, kt
        qh, ql = sb("qh", [P, S], F32R), sb("ql", [P, S], F32R)
        qp = room[:, 0:G, :]
        kp = room[:, G:5 * G, :].rearrange("p (h g) s -> p h g s", h=GH)
        qpm = sb("qpm", [P, 2, S], F32R)
        kh, kl = sb("kh", [P, S], F32R), sb("kl", [P, S], F32R)
        krow = sb("krow", [P, S], F32R)
        nm = sb("nm", [P, 2, T, GH])
        mpad = sb("mpad", [P, T, GH, 32], F32R)
        va = wstage[:, 2 * UNITS * P:].rearrange("p (t h c) -> p t h c", t=T, h=H)
        eb = wstage[:, 0:2 * UNITS * P].rearrange("p (n s) -> p n s", s=2 * S)
        rden = sb("rden", [P, T, GH])
        on = abd
        ov = tcol

        gel, prod = expd[:, 0:2, :], expd[:, 2:4, :]
        act = shifted
        acth, actl = room[:, 2 * T:2 * T + ACTS, :], room[:, 2 * T + ACTS:2 * T + 2 * ACTS, :]
        xh, xl = room[:, 4 * T:4 * T + 2, :], room[:, 4 * T + 2:4 * T + 4, :]
        ocol = ccol

        names = """x_loaded w_loaded ffw_loaded consts_ready passed stat_in stat_ff mv_in mv_ff var_in var_ff rstd_in rstd_ff top_ready pool_link half_ready rs_ready rws_ready wh_ready wl_ready
            link nmax_ready tsum_ready tinv_ready k_ps v_ps kt_ready norm_link mpad_link lg_ready vb_ready normed xt_ps xt_ready bias_added
            q_ps qt_ready v_ready s_ps shift_done exp_done wgt_ready weighted attn_ready abd_ready abd_ps
            abdt_ready c_ps ct_ready o_ps res_a
            normed2 xt2_ps xt2_ready xcols_ready xh_ready xl_ready logit_ps lgn_ready ex8_ready comb_ready comb_ps combt_ready
            combc_ready gates gel_done prod_done cb_ps act_done acth_done actl_done down ocol_ready ot_ps res_f
            bnormed bxt_ps bxt_ready bqkv_ps qv_ready qh_ready ql_ready va_ready krow_ready kp_ready qp_ps qp_ready
            sc_ps sc_max mpad_ready qpm_ps qpm_ready st_ps st_exp pv_done ov_ready on_ps on_ready ont_ps
            ont_ready fc_ps res_b stored zeroed""".split()
        m = {n: sem(n) for n in names}

        block = ctx.enter_context(nc.Block())

        def tile(i, t):
            return res[:, bass.ds(i * T + t, 1), :].rearrange("p a d -> p (a d)")

        def batch(i):
            return res[:, bass.ds(i * T, T), :]

        def at_first(i):
            return isinstance(i, int) and i == 0

        def over_batches(engine, first, body):
            body(first, 0, 0, False, True)
            with engine.Fori(0, (B - 2) // 2) as j:
                for k in range(2):
                    i = j * 2 + 1 + k
                    body(i + first, i, 1 - k, True, True)
            body(first + B - 1, B - 1, 1, True, False)

        def over_tiles(ap2):
            return ap2.unsqueeze(1).to_broadcast([P, T, P])

        @block.sync
        def _(sp):
            x_rows = d["x"].rearrange("(b t p) e -> b p t e", t=T, p=P)
            sp.dma_start(batch(0), x_rows[0]).then_inc(m["x_loaded"], 16)
            with sp.Fori(1, B) as i:
                sp.wait_ge(m["x_loaded"], i * 16)
                sp.dma_start(batch(i), x_rows[bass.ds(i, 1)].rearrange("b p t e -> p (b t) e")).then_inc(m["x_loaded"], 16)
            o_rows = out.rearrange("(b t p) e -> b p t e", t=T, p=P)
            n_res = {1: "res_a", 2: "res_f", 3: "res_b", 4: "res_f"}[stages]
            with sp.Fori(0, B) as i:
                sp.wait_ge(m[n_res], i + 1 + (B if stages == 4 else 0))
                sp.dma_start(o_rows[bass.ds(i, 1)].rearrange("b p t e -> p (b t) e"), batch(i)).then_inc(m["stored"], 16)
            sp.wait_ge(m["stored"], 16 * B)

        @block.vector
        def _(dve):
            link_at = [0]

            def chain(i, per, base):
                k = [0]

                def link(ins, alone=False):
                    ins.then_inc(m["link"], 1)
                    k[0] += 1
                    dve.wait_ge(m["link"], i * per + base + k[0])
                    if alone:
                        dve.sem_inc(m["passed"], 1)
                return link, k

            def statistics(i, n, kind):
                dve.sem_inc(m["passed"], 1)
                for t in range(T):
                    last = dve.bn_stats(stat[kind][:, t, :], tile(i, t))
                last.then_inc(m["stat_" + kind], 1)
                dve.wait_ge(m["stat_" + kind], n + 1)
                dve.sem_inc(m["passed"], 1)
                for t in range(T):
                    last = dve.bn_aggr(mv[kind][:, t, :], stat[kind][:, t, :])
                last.then_inc(m["mv_" + kind], 1)

            def normalised(i, n, kind, done):
                dve.wait_ge(m["rstd_" + kind], n + 1)
                for t in range(T):
                    last = dve.tensor_scalar(xn[kind][:, t, :], tile(i, t), mv[kind][:, t, 0:1], rstd[kind][:, t:t + 1],
                                             ALU.subtract, ALU.mult)
                last.then_inc(m[done], 1)

            def chain(n, done):
                k = [done]

                def link(ins, alone=False):
                    ins.then_inc(m["link"], 1)
                    k[0] += 1
                    dve.wait_ge(m["link"], n * ROUTE_LINKS + k[0])
                    if alone:
                        dve.sem_inc(m["passed"], 1)
                return link, k

            def route_logits(n, products):
                dve.wait_ge(m["rs_ready"], n + 1)
                dve.wait_ge(m["logit_ps"], n + 1)
                dve.tensor_tensor(lg[:, :, :], products[:, 0:T * NE].rearrange("p (t e) -> p t e", e=NE),
                                  rs[:, :].unsqueeze(2).to_broadcast([P, T, NE]), ALU.mult).then_inc(m["lg_ready"], 1)
                dve.wait_ge(m["lg_ready"], n + 1)
                dve.sem_inc(m["passed"], 1)
                for t in range(T):
                    last = dve.max(top[:, t, :], lg[:, t, :])
                last.then_inc(m["top_ready"], 1)
                dve.wait_ge(m["top_ready"], n + 1)
                dve.tensor_tensor(lgn[:, :, :], lg[:, :, :], top[:, :, 0:1].to_broadcast([P, T, NE]),
                                  ALU.subtract).then_inc(m["lgn_ready"], 1)

            def route_choice(n):
                link, k = chain(n, 0)
                for t in range(T):
                    last = dve.max_index(topi[:, t, :], top[:, t, :], lg[:, t, :])
                link(last)
                link(dve.tensor_copy(topf[:, :, :], topi[:, :, 0:2]))
                iota_t = iota[:, :].unsqueeze(1).to_broadcast([P, T, NE])
                dve.tensor_tensor(sel[:, :, :], iota_t, topf[:, :, 0:1].to_broadcast([P, T, NE]), ALU.is_equal)
                link(dve.tensor_tensor(sel2[:, :, :], iota_t, topf[:, :, 1:2].to_broadcast([P, T, NE]), ALU.is_equal))
                link(dve.tensor_tensor(sel[:, :, :], sel[:, :, :], sel2[:, :, :], ALU.add))
                assert k[0] == 4, k[0]

            def route_softmax(n):
                link, k = chain(n, 4)
                dve.wait_ge(m["ex8_ready"], n + 1)
                link(dve.tensor_reduce(tot[:, :], ex8[:, :, :], AX.X, ALU.add))
                link(dve.reciprocal(rec1[:, :], tot[:, :]))
                link(dve.tensor_tensor(comb[:, :, :], ex8[:, :, :], rec1[:, :].unsqueeze(2).to_broadcast([P, T, NE]), ALU.mult))
                link(dve.tensor_tensor(comb[:, :, :], comb[:, :, :], sel[:, :, :], ALU.mult))
                link(dve.tensor_reduce(ren[:, :], comb[:, :, :], AX.X, ALU.add))
                assert k[0] == 9, k[0]

            def route_scaled(i, n):
                link, k = chain(n, 9)
                link(dve.tensor_scalar(low0[:, :], ren[:, :], 0.0, None, ALU.is_le))
                link(dve.tensor_tensor(ren[:, :], ren[:, :], low0[:, :], ALU.max))
                link(dve.reciprocal(rec1[:, :], ren[:, :]))
                link(dve.tensor_tensor(comb[:, :, :], comb[:, :, :], rec1[:, :].unsqueeze(2).to_broadcast([P, T, NE]), ALU.mult))
                link(dve.tensor_tensor(comb[:, :, :], comb[:, :, :], pes[:, :].unsqueeze(1).to_broadcast([P, T, NE]), ALU.mult))
                link(dve.tensor_copy(combh[:, :, :], comb[:, :, :]))
                dve.tensor_copy(comb16[:, bass.ds(i * T, T), 0:NE], combh[:, :, :])
                dve.tensor_tensor(comb16[:, bass.ds(i * T, T), NE:2 * NE], comb[:, :, :], combh[:, :, :], ALU.subtract).then_inc(m["comb_ready"], 1)
                assert k[0] == ROUTE_LINKS, k[0]

            dve.wait_ge(m["w_loaded"], 16 * N_CONST)
            dve.tensor_copy(identr[:, :], ident[:, :])
            dve.tensor_copy(placer[:, :, :, :], place[:, :, :, :])
            dve.tensor_copy(pickr[:, :], pick[:, :])
            dve.memset(mpad[:, :, :, :].rearrange("p t h c -> p (t h c)").bitcast(F32), 0.0).then_inc(m["consts_ready"], 1)
            dve.tensor_scalar(rws[:, :], rw[:, :], cols[:, 5:6], SCALE_A, ALU.mult, ALU.mult).then_inc(m["rws_ready"], 1)

            def scores_shifted(i, t):
                dve.wait_ge(m["s_ps"], i * T + t + 1)
                scores = bank[4 + t][:, :].rearrange("p (m k) -> p m k", k=CHUNK)
                dve.tensor_reduce(nmax[:, t, :], scores, AX.X, ALU.max, negate=True).then_inc(m["nmax_ready"], 1)
                dve.wait_ge(m["nmax_ready"], i * T + t + 1)
                dve.tensor_tensor(shifted[:, t, :].rearrange("p (m k) -> p m k", k=CHUNK), scores,
                                  nmax[:, t, :].unsqueeze(2).to_broadcast([P, NC, CHUNK]), ALU.add).then_inc(m["shift_done"], 1)

            def chunk_weights(i, t):
                dve.wait_ge(m["exp_done"], i * T + t + 1)
                dve.tensor_reduce(tsum[:, t, :], expd[:, t, :].rearrange("p (m k) -> p m k", k=CHUNK), AX.X, ALU.add).then_inc(m["tsum_ready"], 1)
                dve.wait_ge(m["tsum_ready"], i * T + t + 1)
                dve.reciprocal(tsum[:, t, :], tsum[:, t, :]).then_inc(m["tinv_ready"], 1)
                dve.wait_ge(m["tinv_ready"], i * T + t + 1)
                dve.tensor_tensor(wgt[:, t, :], tsum[:, t, :], own[:, t, :], ALU.mult).then_inc(m["wgt_ready"], 1)

            def chunks_summed(i, t):
                dve.wait_ge(m["weighted"], i * T + t + 1)
                dve.tensor_reduce(attn[:, t, :], shifted[:, t, :].rearrange("p (m k) -> p k m", k=CHUNK), AX.X,
                                  ALU.add).then_inc(m["attn_ready"], 1)

            def values_biased(i):
                dve.wait_ge(m["v_ps"], i + 1)
                dve.tensor_tensor(v[:, :, :], bank[1][:, :].rearrange("p (t e) -> p t e", e=P), over_tiles(rows[:, 0, :]),
                                  ALU.add).then_inc(m["v_ready"], 1)

            def chunks_out(i):
                dve.wait_ge(m["o_ps"], i + 1)
                dve.wait_ge(m["bias_added"], i + 1)
                dve.tensor_tensor(batch(i), batch(i), bank[2][:, :].rearrange("p (t e) -> p t e", e=P),
                                  ALU.add).then_inc(m["res_a"], 1)
                dve.wait_ge(m["res_a"], i + 1)
                statistics(i, i, "ff")

            def chunks_batch(i, before, after):
                if after:
                    dve.wait_ge(m["x_loaded"], i * 16 + 32)
                    statistics(i + 1, i + 1, "in")
                scores_shifted(i, 0)
                if after:
                    normalised(i + 1, i + 1, "in", "normed")
                scores_shifted(i, 1)
                chunk_weights(i, 0)
                scores_shifted(i, 2)
                values_biased(i)
                if before:
                    chunks_out(i - 1)
                chunk_weights(i, 1)
                scores_shifted(i, 3)
                chunk_weights(i, 2)
                if before:
                    normalised(i - 1, i - 1, "ff", "normed2")
                chunks_summed(i, 0)
                chunk_weights(i, 3)
                chunks_summed(i, 1)
                if before:
                    route_logits(i - 1, bank[2])
                chunks_summed(i, 2)
                if before:
                    route_choice(i - 1)
                    route_softmax(i - 1)
                chunks_summed(i, 3)
                if before:
                    route_scaled(i - 1, i - 1)

            dve.wait_ge(m["x_loaded"], 16)
            statistics(0, 0, "in")
            normalised(0, 0, "in", "normed")
            chunks_batch(0, False, True)
            with dve.Fori(1, B - 1) as i:
                chunks_batch(i, True, True)
            chunks_batch(B - 1, True, False)
            chunks_out(B - 1)
            normalised(B - 1, B - 1, "ff", "normed2")
            route_logits(B - 1, bank[2])
            route_choice(B - 1)
            route_softmax(B - 1)
            route_scaled(B - 1, B - 1)

            dve.wait_ge(m["wh_ready"], 1)
            dve.tensor_tensor(wl[:, :], wstage[:, :], wh[:, :], ALU.subtract).then_inc(m["wl_ready"], 1)
            dve.wait_ge(m["wl_ready"], 1)
            dve.memset(wstage[:, 2 * UNITS * P:], 0.0).then_inc(m["zeroed"], 1)
            dve.wait_ge(m["zeroed"], 1)
            dve.memset(va[:, :, :, HD:HD + 1], 1.0)

            def ff_batch(n, i, parity, before, after):
                for u in range(UNITS):
                    dve.wait_ge(m["gel_done"], n * UNITS + u + 1)
                    dve.tensor_tensor(prod[:, u % 2, :], bank[2 + u % 2][:, :], gel[:, u % 2, :], ALU.mult).then_inc(m["prod_done"], 1)
                    if u % 2 == 0:
                        dve.wait_ge(m["cb_ps"], n * NE + u // 2 + 1)
                    dve.wait_ge(m["prod_done"], n * UNITS + u + 1)
                    if u >= ACTS or before:
                        dve.wait_ge(m["actl_done"], n * UNITS + u - ACTS + 1)
                    dve.tensor_tensor(act[:, u % ACTS, :], bank[4 + (u // 2) % 2][:, :], prod[:, u % 2, :], ALU.mult).then_inc(m["act_done"], 1)
                    if u == AHEAD + 2 and before:
                        ff_out(n - 1, i - 1)

            def ff_out(n, i):
                dve.wait_ge(m["ot_ps"], n + 1)
                dve.tensor_tensor(batch(i), batch(i), bank[7][:, :].rearrange("p (t e) -> p t e", e=P),
                                  ALU.add).then_inc(m["res_f"], 1)

            def feed_forward(first):
                over_batches(dve, first, ff_batch)
                ff_out(first + B - 1, B - 1)
            if stages >= 2:
                feed_forward(0)
            def maxima(i, at, half):
                for hh in (2 * half, 2 * half + 1):
                    n = i * (H * T) + at * GH + hh
                    dve.wait_ge(m["sc_ps"], n + 1)
                    dve.tensor_reduce(nm[:, at // T % 2, at % T, hh:hh + 1], bank[hh % 2][:, :], AX.X, ALU.max, negate=True).then_inc(m["sc_max"], 1)

            def maxima_rows(b, g):
                dve.wait_ge(m["sc_max"], b * (H * T) + (g + 1) * T * GH)
                if not (at_first(b) and g == 0):
                    dve.wait_ge(m["qpm_ps"], b * G + g)
                    dve.wait_ge(m["mpad_ready"], b * G + g)
                dve.tensor_copy(mpad[:, :, :, ONE], nm[:, g % 2, :, :]).then_inc(m["mpad_link"], 1)
                dve.wait_ge(m["mpad_link"], b * G + g + 1)
                dve.tensor_tensor(mpad[:, :, :, ONE + 1], nm[:, g % 2, :, :], mpad[:, :, :, ONE], ALU.subtract).then_inc(m["mpad_ready"], 1)

            def normalise(b, g):
                dve.wait_ge(m["on_ps"], b * G + g + 1)
                sums = bank[7][:, :].rearrange("p (t h c) -> p t h c", h=GH, c=32)
                dve.reciprocal(rden[:, :, :], sums[:, :, :, HD]).then_inc(m["norm_link"], 1)
                dve.wait_ge(m["norm_link"], b * G + g + 1)
                for t in range(T):
                    last = dve.tensor_tensor(on[:, t, g * 32:g * 32 + 32].rearrange("p (h j) -> p h j", j=HD), sums[:, t, :, 0:HD],
                                             rden[:, t, :].unsqueeze(2).to_broadcast([P, GH, HD]), ALU.mult)
                last.then_inc(m["on_ready"], 1)

            def head_rows(b, n, bias):
                dve.wait_ge(m["bqkv_ps"], b * 3 + n + 1)
                dve.tensor_scalar((qv, kv)[n][:, :], bank[7][:, :], cols[:, bias:bias + 1], cols[:, 4:5], ALU.add, ALU.mult).then_inc(m["qv_ready"], 1)

            def values_in(b):
                dve.wait_ge(m["bqkv_ps"], b * 3 + 3)
                dve.tensor_tensor(v[:, :, :], bank[7][:, :].rearrange("p (t e) -> p t e", e=P), over_tiles(rows[:, 2, :]), ALU.add).then_inc(m["vb_ready"], 1)

            def values_placed(b, g, first=False):
                dve.wait_ge(m["vb_ready"], b + 1)
                if not first:
                    dve.wait_ge(m["pv_done"], b * (G * T) - (G - 1 - g) * T)
                heads = slice(g * GH, (g + 1) * GH)
                dve.tensor_tensor(va[:, :, heads, 0:HD], v[:, :, g * 32:g * 32 + 32].rearrange("p t (h j) -> p t h j", j=HD),
                                  rows[:, 4, g * 32:g * 32 + 32].rearrange("p (h j) -> p h j", j=HD).unsqueeze(1).to_broadcast([P, T, GH, HD]),
                                  ALU.mult).then_inc(m["va_ready"], 1)

            def heads_out(b):
                dve.wait_ge(m["fc_ps"], b + 1)
                dve.wait_ge(m["bias_added"], B + b + 1)
                dve.tensor_tensor(batch(b), batch(b), bank[7][:, :].rearrange("p (t e) -> p t e", e=P), ALU.add).then_inc(m["res_b"], 1)

            def finish_at(b, at, prepared=False):
                if at == (1, 0):
                    normalise(b, G - 1)
                if at == (4, 0):
                    heads_out(b)
                if at == (5, 0):
                    dve.wait_ge(m["res_b"], b + 1)
                    statistics(b, b + B, "ff")
                if at == (7, 0):
                    normalised(b, b + B, "ff", "normed2")
                if at == (10, 0):
                    route_logits(b + B, bank[7])
                if at == (11, 0):
                    route_choice(b + B)
                if at == (12, 0):
                    route_softmax(b + B)
                if at == (14, 1):
                    route_scaled(b, b + B)

            def prepare_at(b, at):
                if at == (0, 1):
                    statistics(b, b + B, "in")
                if at == (2, 0):
                    normalised(b, b + B, "in", "bnormed")
                if at == (4, 1):
                    head_rows(b, 0, 2)
                if at == (5, 1):
                    head_rows(b, 1, 3)
                if at == (6, 0):
                    values_in(b)
                if at in ((7, 1), (10, 1), (14, 0)):
                    values_placed(b, {7: 0, 10: 1, 14: 2}[at[0]])

            def heads_batch(i, finish, prepare):
                for at in ((s, half) for s in range(STEPS) for half in range(2)):
                    s, half = at
                    if s + LEAD < STEPS or prepare:
                        maxima(i, s + LEAD, half)
                    if at in ((5, 0), (9, 0), (13, 0)):
                        normalise(i, s // T - 1)
                    if finish:
                        finish_at(i - 1, at, prepare)
                    if prepare:
                        prepare_at(i + 1, at)
                    if at in ((1, 1), (5, 1), (9, 1)):
                        maxima_rows(i, s // T + 1)
                    if at == (13, 1) and prepare:
                        maxima_rows(i + 1, 0)
                    if at == (2, 1) and finish:
                        values_placed(i, G - 1)

            if stages >= 3:
                for at in ((0, 1), (2, 0), (4, 1), (5, 1), (6, 0)):
                    prepare_at(0, at)
                for g in range(G):
                    values_placed(0, g, first=True)
                for k in range(LEAD):
                    for half in range(2):
                        maxima(0, k, half)
                    if k == T - 1:
                        maxima_rows(0, 0)
                heads_batch(0, False, True)
                with dve.Fori(1, B - 1) as i:
                    heads_batch(i, True, True)
                heads_batch(B - 1, True, False)
                for at in ((1, 0), (4, 0), (5, 0), (7, 0), (10, 0), (11, 0), (12, 0), (14, 1)):
                    finish_at(B - 1, at)
            if stages >= 4:
                feed_forward(B)

        @block.scalar
        def _(act_e):
            small = [(wq, "wq"), (wk, "wk"), (wv, "wv"), (wo, "wo"), (wqb, "wqb"), (wkb, "wkb"), (wvb, "wvb"), (wfc, "wfc"),
                     (cols, "cols"), (rw, "rw"), (ident, "ident")]
            for dst, name in small:
                act_e.dma_start(dst[:, :], d[name]).then_inc(m["w_loaded"], 16)
            act_e.dma_start(rows[:, :, :], d["rows"].unsqueeze(0).to_broadcast([P, 5, P])).then_inc(m["w_loaded"], 16)
            act_e.dma_start(pes[:, :], d["pes"].unsqueeze(0).to_broadcast([P, NE])).then_inc(m["w_loaded"], 16)
            act_e.dma_start(own[:, :, :], d["own"]).then_inc(m["w_loaded"], 16)
            act_e.dma_start(block_mask[:, :, :], d["block_mask"]).then_inc(m["w_loaded"], 16)
            act_e.dma_start(iota[:, :], d["iota"]).then_inc(m["w_loaded"], 16)
            act_e.dma_start(place[:, :, :, :], d["place"]).then_inc(m["w_loaded"], 16)
            act_e.dma_start(pick[:, :], d["pick"]).then_inc(m["w_loaded"], 16)
            act_e.dma_start(wstage[:, 0:2 * UNITS * P], d["wgate"]).then_inc(m["ffw_loaded"], 16)
            act_e.dma_start(wstage[:, 2 * UNITS * P:], d["wdown"]).then_inc(m["ffw_loaded"], 16)

            def copy(dst, src):
                return act_e.activation(dst, src, ACT.Copy)

            def routed_columns(n, side):
                act_e.wait_ge(m["xt2_ps"], n + 1)
                if not at_first(n):
                    act_e.wait_ge(m["xcols_ready"], n)
                copy(xt["ff"][:, :], side).then_inc(m["xt2_ready"], 1)

            def routed_exponentials(n):
                act_e.wait_ge(m["lgn_ready"], n + 1)
                act_e.activation(ex8[:, :, :], lgn[:, :, :], ACT.Exp).then_inc(m["ex8_ready"], 1)

            def chunks_columns(i):
                act_e.wait_ge(m["xt_ps"], i + 1)
                copy(xt["in"][:, :], bank[0][:, :]).then_inc(m["xt_ready"], 1)

            def chunks_queries(i):
                act_e.wait_ge(m["q_ps"], i + 1)
                act_e.activation(qt[:, :], bank[1][:, :], ACT.Identity, bias=cols[:, 0:1]).then_inc(m["qt_ready"], 1)

            def chunks_keys(i):
                act_e.wait_ge(m["k_ps"], i + 1)
                act_e.activation(kt[:, :], bank[0][:, :], ACT.Identity, bias=cols[:, 1:2]).then_inc(m["kt_ready"], 1)

            def chunks_exponentials(i, t):
                act_e.wait_ge(m["shift_done"], i * T + t + 1)
                act_e.activation(expd[:, t, :], shifted[:, t, :], ACT.Exp, scale=SCALE_A).then_inc(m["exp_done"], 1)

            def attention_columns(i):
                act_e.wait_ge(m["abd_ps"], i + 1)
                copy(tcol[:, :], bank[2][:, :]).then_inc(m["abdt_ready"], 1)

            def combined_columns(i):
                act_e.wait_ge(m["c_ps"], i + 1)
                copy(ccol[:, :], bank[3][:, :]).then_inc(m["ct_ready"], 1)

            def chunks_batch(i, before, after):
                if before:
                    attention_columns(i - 1)
                chunks_exponentials(i, 0)
                if before:
                    combined_columns(i - 1)
                chunks_exponentials(i, 1)
                if after:
                    chunks_columns(i + 1)
                if after:
                    chunks_queries(i + 1)
                chunks_exponentials(i, 2)
                if after:
                    chunks_keys(i + 1)
                chunks_exponentials(i, 3)
                if before:
                    routed_columns(i - 1, bank[3][:, :])
                    routed_exponentials(i - 1)

            act_e.wait_ge(m["w_loaded"], 16 * N_CONST)
            chunks_columns(0)
            chunks_queries(0)
            chunks_keys(0)
            chunks_batch(0, False, True)
            with act_e.Fori(1, B - 1) as i:
                chunks_batch(i, True, True)
            chunks_batch(B - 1, True, False)
            attention_columns(B - 1)
            combined_columns(B - 1)
            routed_columns(B - 1, bank[3][:, :])
            routed_exponentials(B - 1)
            act_e.wait_ge(m["ffw_loaded"], 32)
            copy(wh[:, :], wstage[:, :]).then_inc(m["wh_ready"], 1)

            def ff_columns(n, i, parity):
                copy(xh[:, parity, :], xcols[:, bass.ds(i * S, S)]).then_inc(m["xh_ready"], 1)

            def ff_weights(n, i):
                act_e.wait_ge(m["comb_ready"], n + 1)
                copy(combc[:, :, :], comb16[:, bass.ds(i * T, T), :]).then_inc(m["combc_ready"], 1)

            def ff_weight_columns(n):
                act_e.wait_ge(m["comb_ps"], n + 1)
                copy(combt[:, :], bank[7][0:2 * NE, :]).then_inc(m["combt_ready"], 1)

            def ff_high(n, u):
                act_e.wait_ge(m["act_done"], n * UNITS + u + 1)
                copy(acth[:, u % ACTS, :], act[:, u % ACTS, :]).then_inc(m["acth_done"], 1)

            def ff_out(n):
                act_e.wait_ge(m["down"], n * UNITS)
                copy(ocol[:, :], bank[6][:, :]).then_inc(m["ocol_ready"], 1)

            def ff_batch(n, i, parity, before, after):
                for u in range(UNITS):
                    if u == AHEAD and before:
                        ff_out(n)
                    act_e.wait_ge(m["gates"], n * UNITS + u + 1)
                    act_e.activation(gel[:, u % 2, :], bank[u % 2][:, :], ACT.Gelu_apprx_tanh).then_inc(m["gel_done"], 1)
                    if u >= 1 or before:
                        if u > ACTS or before:
                            act_e.wait_ge(m["down"], n * UNITS + u - ACTS)
                        ff_high(n, u - 1) if u else ff_high(n - 1, UNITS - 1)
                    if after and u == 8:
                        ff_columns(n + 1, i + 1, 1 - parity)
                    if after and u == 9:
                        ff_weights(n + 1, i + 1)
                if after:
                    act_e.wait_ge(m["cb_ps"], (n + 1) * NE)
                    ff_weight_columns(n + 1)

            def feed_forward(first):
                act_e.wait_ge(m["xcols_ready"], first + B)
                ff_columns(first, 0, 0)
                ff_weights(first, 0)
                ff_weight_columns(first)
                over_batches(act_e, first, ff_batch)
                ff_high(first + B - 1, UNITS - 1)
                ff_out(first + B)
            if stages >= 2:
                feed_forward(0)
            def placed(b, g, part):
                act_e.wait_ge(m["qp_ps"], b * 2 * G + 2 * g + part + 1)
                if part == 0:
                    copy(qp[:, g, :], bank[7][:, :]).then_inc(m["qp_ready"], 1)
                else:
                    if not (at_first(b) and g == 0):
                        act_e.wait_ge(m["kp_ready"], (b * G + g) * GH)
                    act_e.activation(krow[:, :], bank[7][:, :], ACT.Identity, bias=cols[:, 6 + GH:7 + GH]).then_inc(m["krow_ready"], 1)

            def exponentials(i, s, pair):
                gs = i * STEPS + s
                n = 2 * s + pair
                act_e.wait_ge(m["st_ps"], gs * 2 + pair + 1)
                if not (at_first(i) and n < EBUFS):
                    act_e.wait_ge(m["pv_done"], gs + (pair - EBUFS) // 2 + 1)
                two = KEY_BANKS[pair]
                act_e.activation(eb[:, n % EBUFS, :], banks[:, two:two + 2, :].rearrange("p a s -> p (a s)"),
                                 ACT.Exp, scale=SCALE_B).then_inc(m["st_exp"], 1)

            def maxima_in(b, g):
                act_e.wait_ge(m["qpm_ps"], b * G + g + 1)
                copy(qpm[:, g % 2, :], bank[7][:, :]).then_inc(m["qpm_ready"], 1)

            def sums_out(b, g):
                act_e.wait_ge(m["pv_done"], b * (G * T) + (g + 1) * T)
                copy(ov[:, :], bank[6][:, :]).then_inc(m["ov_ready"], 1)

            def finish_at(b, at):
                if at == (0, 0):
                    sums_out(b, G - 1)
                if at == (3, 0):
                    act_e.wait_ge(m["ont_ps"], b + 1)
                    copy(ccol[:, :], bank[7][:, :]).then_inc(m["ont_ready"], 1)
                if at == (8, 0):
                    routed_columns(b + B, bank[7][:, :])
                if at == (11, 0):
                    routed_exponentials(b + B)

            def prepare_at(b, at):
                if at == (3, 1):
                    act_e.wait_ge(m["bxt_ps"], b + 1)
                    copy(xt["in"][:, :], bank[7][:, :]).then_inc(m["bxt_ready"], 1)
                if at == (5, 0):
                    act_e.wait_ge(m["qv_ready"], b * 2 + 1)
                    copy(qh[:, :], qv[:, :]).then_inc(m["qh_ready"], 1)
                if at == (6, 0):
                    act_e.wait_ge(m["qv_ready"], b * 2 + 2)
                    copy(kh[:, :], kv[:, :]).then_inc(m["qh_ready"], 1)
                if at in PLACED:
                    placed(b, *PLACED[at])

            def heads_batch(i, finish, prepare):
                for at in ((s, half) for s in range(STEPS) for half in range(2)):
                    s, half = at
                    exponentials(i, s, half)
                    if at in ((4, 0), (8, 0), (12, 0)):
                        sums_out(i, s // T - 1)
                    if finish:
                        finish_at(i - 1, at)
                    if at in LATE:
                        placed(i, G - 1, half)
                    if prepare:
                        prepare_at(i + 1, at)
                    if at in ((2, 1), (6, 1), (10, 1)):
                        maxima_in(i, s // T + 1)
                    if at == (14, 1) and prepare:
                        maxima_in(i + 1, 0)

            if stages >= 3:
                for at in ((3, 1), (5, 0), (6, 0), *PLACED):
                    prepare_at(0, at)
                maxima_in(0, 0)
                heads_batch(0, False, True)
                with act_e.Fori(1, B - 1) as i:
                    heads_batch(i, True, True)
                heads_batch(B - 1, True, False)
                for at in ((0, 0), (3, 0), (8, 0), (11, 0)):
                    finish_at(B - 1, at)
            if stages >= 4:
                feed_forward(B)

        @block.gpsimd
        def _(pool):
            for n, value in enumerate((-0.5, 1e-5, 1e-6)):
                pool.memset(consts[:, n, :], value).then_inc(m["half_ready"], 1)
            pool.wait_ge(m["w_loaded"], 16 * N_CONST)
            pool.wait_ge(m["half_ready"], 3)

            def deviation(n, kind):
                pool.wait_ge(m["mv_" + kind], n + 1)
                pool.tensor_tensor(rstd[kind][:, :], mv[kind][:, :, 1], consts[:, 1, :], ALU.add).then_inc(m["var_" + kind], 1)
                pool.wait_ge(m["var_" + kind], n + 1)
                pool.tensor_tensor(rstd[kind][:, :], rstd[kind][:, :], consts[:, 0, :], ALU.pow).then_inc(m["rstd_" + kind], 1)

            def route_deviation(n):
                deviation(n, "ff")
                pool.wait_ge(m["rstd_ff"], n + 1)
                for k, (in0, in1, op) in enumerate(((rstd["ff"][:, :], rstd["ff"][:, :], ALU.mult), (rs[:, :], mv["ff"][:, :, 1], ALU.mult),
                                                    (rs[:, :], consts[:, 2, :], ALU.add))):
                    pool.tensor_tensor(rs[:, :], in0, in1, op).then_inc(m["pool_link"], 1)
                    pool.wait_ge(m["pool_link"], n * 3 + k + 1)
                pool.tensor_tensor(rs[:, :], rs[:, :], consts[:, 0, :], ALU.pow).then_inc(m["rs_ready"], 1)

            def route(i, n):
                pool.wait_ge(m["xt2_ready"], n + 1)
                pool.tensor_copy(xcols[:, bass.ds(i * S, S)], xt["ff"][:, :]).then_inc(m["xcols_ready"], 1)

            def bias_added(i):
                pool.wait_ge(m["normed"], i + 1)
                pool.tensor_tensor(batch(i), batch(i), over_tiles(rows[:, 1, :]), ALU.add).then_inc(m["bias_added"], 1)

            def weighted(i, t):
                pool.wait_ge(m["wgt_ready"], i * T + t + 1)
                pool.tensor_tensor(shifted[:, t, :].rearrange("p (m k) -> p m k", k=CHUNK),
                                   expd[:, t, :].rearrange("p (m k) -> p m k", k=CHUNK),
                                   wgt[:, t, :].unsqueeze(2).to_broadcast([P, NC, CHUNK]), ALU.mult).then_inc(m["weighted"], 1)

            def block_diagonal(i, t):
                pool.wait_ge(m["attn_ready"], i * T + t + 1)
                pool.tensor_tensor(abd[:, t, :].rearrange("p (c k) -> p c k", k=CHUNK), block_mask[:, :, :],
                                   attn[:, t, :].unsqueeze(1).to_broadcast([P, T, CHUNK]), ALU.mult).then_inc(m["abd_ready"], 1)

            def chunks_batch(i, before, after):
                if after:
                    deviation(i + 1, "in")
                weighted(i, 0)
                if after:
                    bias_added(i + 1)
                weighted(i, 1)
                if before:
                    route_deviation(i - 1)
                weighted(i, 2)
                block_diagonal(i, 0)
                weighted(i, 3)
                block_diagonal(i, 1)
                block_diagonal(i, 2)
                block_diagonal(i, 3)
                if before:
                    route(i - 1, i - 1)

            deviation(0, "in")
            bias_added(0)
            chunks_batch(0, False, True)
            with pool.Fori(1, B - 1) as i:
                chunks_batch(i, True, True)
            chunks_batch(B - 1, True, False)
            route_deviation(B - 1)
            route(B - 1, B - 1)

            def ff_columns(n, i, parity):
                pool.wait_ge(m["xh_ready"], n + 1)
                pool.tensor_tensor(xl[:, parity, :], xcols[:, bass.ds(i * S, S)], xh[:, parity, :], ALU.subtract).then_inc(m["xl_ready"], 1)

            def ff_batch(n, i, parity, before, after):
                for u in range(UNITS):
                    pool.wait_ge(m["acth_done"], n * UNITS + u + 1)
                    pool.tensor_tensor(actl[:, u % ACTS, :], act[:, u % ACTS, :], acth[:, u % ACTS, :],
                                       ALU.subtract).then_inc(m["actl_done"], 1)
                    if after and u == 8:
                        ff_columns(n + 1, i + 1, 1 - parity)

            def feed_forward(first):
                ff_columns(first, 0, 0)
                over_batches(pool, first, ff_batch)
            if stages >= 2:
                feed_forward(0)
            def prepare(b):
                deviation(b + B, "in")
                pool.wait_ge(m["bnormed"], b + 1)
                pool.tensor_tensor(batch(b), batch(b), over_tiles(rows[:, 3, :]), ALU.add).then_inc(m["bias_added"], 1)

            def split(b):
                pool.wait_ge(m["qh_ready"], b * 2 + 1)
                pool.tensor_tensor(ql[:, :], qv[:, :], qh[:, :], ALU.subtract).then_inc(m["ql_ready"], 1)
                pool.wait_ge(m["qh_ready"], b * 2 + 2)
                pool.tensor_tensor(kl[:, :], kv[:, :], kh[:, :], ALU.subtract).then_inc(m["ql_ready"], 1)

            def keys_placed(b, g):
                pool.wait_ge(m["krow_ready"], b * G + g + 1)
                for hh in range(GH):
                    pool.tensor_tensor(kp[:, hh, g, :], krow[:, :], cols[:, 6 + hh:7 + hh].to_broadcast([P, S]), ALU.mult).then_inc(m["kp_ready"], 1)

            if stages >= 3:
                prepare(0)
                split(0)
                for g in range(G - 1):
                    keys_placed(0, g)
                keys_placed(0, G - 1)
                prepare(1)
                split(1)
                for g in range(G - 1):
                    keys_placed(1, g)
                with pool.Fori(1, B - 1) as i:
                    prepare(i + 1)
                    keys_placed(i, G - 1)
                    route_deviation(i - 1 + B)
                    split(i + 1)
                    keys_placed(i + 1, 0)
                    route(i - 1, i - 1 + B)
                    keys_placed(i + 1, 1)
                    keys_placed(i + 1, 2)
                keys_placed(B - 1, G - 1)
                for b in (B - 2, B - 1):
                    route_deviation(b + B)
                    route(b, b + B)
            if stages >= 4:
                feed_forward(B)

        @block.tensor
        def _(pe):
            pe.wait_ge(m["w_loaded"], 16 * N_CONST)
            pe.wait_ge(m["consts_ready"], 1)
            pe.wait_ge(m["rws_ready"], 1)

            def transposes(to, src, rows_out=P):
                for t in range(T):
                    last = pe.transpose(to[0:rows_out, t * P:(t + 1) * P], src[:, t, :], ident[:, :])
                return last

            def by_tile(to, columns, w):
                for t in range(T):
                    last = pe.matmul(to[:, t * P:(t + 1) * P], columns[:, t * P:(t + 1) * P], w, start=True, stop=True)
                return last

            def logits(n, to):
                pe.wait_ge(m["xt2_ready"], n + 1)
                for t in range(T):
                    last = pe.matmul(to[:, t * NE:(t + 1) * NE], xt["ff"][:, t * P:(t + 1) * P], rws[:, :], start=True, stop=True)
                last.then_inc(m["logit_ps"], 1)

            def chunks_columns(i):
                pe.wait_ge(m["normed"], i + 1)
                transposes(bank[0], xn["in"]).then_inc(m["xt_ps"], 1)

            def chunks_queries(i):
                pe.wait_ge(m["xt_ready"], i + 1)
                if not at_first(i):
                    pe.wait_ge(m["v_ready"], i)
                pe.matmul(bank[1][:, :], wq[:, :], xt["in"][:, :], start=True, stop=True).then_inc(m["q_ps"], 1)

            def chunks_keys(i):
                pe.matmul(bank[0][:, :], wk[:, :], xt["in"][:, :], start=True, stop=True).then_inc(m["k_ps"], 1)

            def chunks_values(i):
                by_tile(bank[1], xt["in"], wv[:, :]).then_inc(m["v_ps"], 1)

            def chunks_scores(i, t):
                if not at_first(i):
                    pe.wait_ge(m["shift_done"], i * T + t + 1 - T)
                pe.matmul(bank[4 + t][:, :], qt[:, t * P:(t + 1) * P], kt[:, :], start=True, stop=True).then_inc(m["s_ps"], 1)

            def attention_columns(i):
                pe.wait_ge(m["abd_ready"], i * T + T)
                if not at_first(i):
                    pe.wait_ge(m["lg_ready"], i)
                transposes(bank[2], abd).then_inc(m["abd_ps"], 1)

            def combined(i):
                pe.wait_ge(m["abdt_ready"], i + 1)
                pe.wait_ge(m["v_ready"], i + 1)
                for t in range(T):
                    last = pe.matmul(bank[3][:, t * P:(t + 1) * P], v[:, t, :], tcol[:, t * P:(t + 1) * P], start=True, stop=True)
                last.then_inc(m["c_ps"], 1)

            def chunks_out(i):
                pe.wait_ge(m["ct_ready"], i + 1)
                by_tile(bank[2], ccol, wo[:, :]).then_inc(m["o_ps"], 1)

            def routed(i):
                pe.wait_ge(m["normed2"], i + 1)
                transposes(bank[3], xn["ff"]).then_inc(m["xt2_ps"], 1)
                logits(i, bank[2])

            def chunks_batch(i, before, after):
                pe.wait_ge(m["qt_ready"], i + 1)
                pe.wait_ge(m["kt_ready"], i + 1)
                chunks_scores(i, 0)
                chunks_scores(i, 1)
                if before:
                    attention_columns(i - 1)
                chunks_scores(i, 2)
                if before:
                    combined(i - 1)
                chunks_scores(i, 3)
                chunks_values(i)
                if before:
                    chunks_out(i - 1)
                if after:
                    chunks_columns(i + 1)
                if after:
                    chunks_queries(i + 1)
                    chunks_keys(i + 1)
                if before:
                    routed(i - 1)

            chunks_columns(0)
            chunks_queries(0)
            chunks_keys(0)
            chunks_batch(0, False, True)
            with pe.Fori(1, B - 1) as i:
                chunks_batch(i, True, True)
            chunks_batch(B - 1, True, False)
            attention_columns(B - 1)
            combined(B - 1)
            chunks_out(B - 1)
            routed(B - 1)

            def three(to, w0, high, low, start, stop):
                pe.matmul(to, wh[:, w0:w0 + P], high, start=start, stop=False)
                pe.matmul(to, wh[:, w0:w0 + P], low, start=False, stop=False)
                return pe.matmul(to, wl[:, w0:w0 + P], high, start=False, stop=stop)

            def ff_weight_columns(n):
                pe.wait_ge(m["combc_ready"], n + 1)
                transposes(bank[7], combc, 2 * NE).then_inc(m["comb_ps"], 1)

            def ff_down(n, u):
                pe.wait_ge(m["actl_done"], n * UNITS + u + 1)
                three(bank[6][:, :], (2 * UNITS + u) * P, acth[:, u % ACTS, :], actl[:, u % ACTS, :],
                      u == 0, u == UNITS - 1).then_inc(m["down"], 1)

            def ff_out(n):
                pe.wait_ge(m["ocol_ready"], n + 1)
                for t in range(T):
                    last = pe.transpose(bank[7][:, t * P:(t + 1) * P], ocol[:, t * P:(t + 1) * P], ident[:, :])
                last.then_inc(m["ot_ps"], 1)

            def ff_batch(n, i, parity, before, after):
                pe.wait_ge(m["xl_ready"], n + 1)
                for u in range(UNITS):
                    if u >= 2 or before:
                        pe.wait_ge(m["prod_done"], n * UNITS + u - 1)
                    high, low = xh[:, parity, :], xl[:, parity, :]
                    three(bank[u % 2][:, :], u * P, high, low, True, True)
                    three(bank[2 + u % 2][:, :], (UNITS + u) * P, high, low, True, True).then_inc(m["gates"], 1)
                    if u % 2 == 0:
                        if u == 0:
                            pe.wait_ge(m["combt_ready"], n + 1)
                        if u >= 4 or before:
                            pe.wait_ge(m["act_done"], n * UNITS + u - 2)
                        pe.matmul(bank[4 + (u // 2) % 2][:, :], pickr[:, u // 2:u // 2 + 1].to_broadcast([2 * NE, P]), combt[:, :],
                                  start=True, stop=True).then_inc(m["cb_ps"], 1)
                    if u < AHEAD and before:
                        ff_down(n - 1, UNITS + u - AHEAD)
                    if u >= AHEAD:
                        if u == AHEAD and before:
                            pe.wait_ge(m["ocol_ready"], n)
                        ff_down(n, u - AHEAD)
                    if u == AHEAD + 1 and before:
                        ff_out(n - 1)
                    if u == 11 and after:
                        if before:
                            pe.wait_ge(m["res_f"], n)
                        ff_weight_columns(n + 1)

            def feed_forward(first):
                pe.wait_ge(m["wl_ready"], 1)
                pe.wait_ge(m["comb_ready"], first + B)
                ff_weight_columns(first)
                over_batches(pe, first, ff_batch)
                n = first + B - 1
                for u in range(UNITS - AHEAD, UNITS):
                    ff_down(n, u)
                ff_out(n)
                pe.wait_ge(m["res_f"], n + 1)
            if stages >= 2:
                feed_forward(0)
            side = [None]

            def side_free():
                if side[0] is not None:
                    pe.wait_ge(m[side[0][0]], side[0][1])

            def side_used(name, count):
                side[0] = (name, count)

            def place_rows(b, g, part):
                side_free()
                hi, lo = ((qh, ql), (kh, kl))[part]
                pe.wait_ge(m["ql_ready"], b * 2 + part + 1)
                pe.matmul(bank[7][:, :], placer[:, 2 * part, g, :], hi[:, :], start=True, stop=False)
                pe.matmul(bank[7][:, :], placer[:, 2 * part + 1, g, :], lo[:, :], start=False, stop=True).then_inc(m["qp_ps"], 1)
                side_used(("qp_ready", "krow_ready")[part], b * G + g + 1)

            def score(i, at, hh):
                g, t = at // T % G, at % T
                n = i * (H * T) + at * GH + hh
                if not (at_first(i) and at * GH + hh < 2):
                    pe.wait_ge(m["sc_max"], n - 1)
                pe.matmul(bank[hh % 2][:, :], qp[:, g, t * P:(t + 1) * P], kp[:, hh, g, :],
                          start=True, stop=True).then_inc(m["sc_ps"], 1)

            def max_rows(b, g):
                side_free()
                pe.wait_ge(m["mpad_ready"], b * G + g + 1)
                pe.matmul(bank[7][:, :], identr[:, :], qp[:, g, :], start=True, stop=False)
                for t in range(T):
                    last = pe.matmul(bank[7][:, t * P:(t + 1) * P], mpad[:, t, :, :].rearrange("p h c -> p (h c)"), identr[:, :],
                                     start=False, stop=t == T - 1)
                last.then_inc(m["qpm_ps"], 1)
                side_used("qpm_ready", b * G + g + 1)

            def keys(i, s, hh):
                g, t, pair = s // T, s % T, hh // 2
                if hh % 2 == 0 and not (at_first(i) and s == 0):
                    pe.wait_ge(m["st_exp"], (i * STEPS + s) * 2 + pair - 1)
                last = pe.matmul(bank[KEY_BANKS[pair] + hh % 2][:, :], kp[:, hh, g, t * P:(t + 1) * P], qpm[:, g % 2, :],
                                 start=True, stop=True)
                if hh % 2:
                    last.then_inc(m["st_ps"], 1)

            def values(i, s):
                g, t = s // T % G, s % T
                pe.wait_ge(m["st_exp"], (i * STEPS + s) * 2 + 2)
                if t == 0 and not (at_first(i) and s == 0):
                    pe.wait_ge(m["ov_ready"], i * G + s // T)
                for hh in range(GH):
                    n = 2 * s + hh // 2
                    last = pe.matmul(bank[6][32 * hh:32 * hh + 32, :], va[:, t, g * GH + hh, :],
                                     eb[:, n % EBUFS, (hh % 2) * S:(hh % 2 + 1) * S], start=t == 0, stop=t == T - 1,
                                     tile_position=(0, 32 * hh))
                last.then_inc(m["pv_done"], 1)

            def to_rows(b, g):
                side_free()
                pe.wait_ge(m["ov_ready"], b * G + g + 1)
                for t in range(T):
                    last = pe.transpose(bank[7][:, t * P:(t + 1) * P], ov[:, t * P:(t + 1) * P], ident[:, :])
                last.then_inc(m["on_ps"], 1)
                side_used("on_ready", b * G + g + 1)

            def group_placed(b, g):
                pe.wait_ge(m["qp_ready"], b * G + g + 1)
                pe.wait_ge(m["kp_ready"], (b * G + g + 1) * GH)

            def finish_at(b, at):
                if at == (1, 0):
                    to_rows(b, G - 1)
                if at == (3, 0):
                    side_free()
                    pe.wait_ge(m["on_ready"], b * G + G)
                    transposes(bank[7], on).then_inc(m["ont_ps"], 1)
                    side_used("ont_ready", b + 1)
                if at == (4, 0):
                    side_free()
                    pe.wait_ge(m["ont_ready"], b + 1)
                    by_tile(bank[7], ccol, wfc[:, :]).then_inc(m["fc_ps"], 1)
                    side_used("res_b", b + 1)
                if at == (8, 0):
                    side_free()
                    pe.wait_ge(m["normed2"], b + B + 1)
                    transposes(bank[7], xn["ff"]).then_inc(m["xt2_ps"], 1)
                    side_used("xt2_ready", b + B + 1)
                if at == (10, 0):
                    side_free()
                    logits(b + B, bank[7])
                    side_used("lg_ready", b + B + 1)

            def prepare_at(b, at):
                if at == (3, 1):
                    side_free()
                    pe.wait_ge(m["bnormed"], b + 1)
                    transposes(bank[7], xn["in"]).then_inc(m["bxt_ps"], 1)
                    side_used("bxt_ready", b + 1)
                if at in ((4, 1), (5, 1)):
                    side_free()
                    pe.wait_ge(m["bxt_ready"], b + 1)
                    n = at[0] - 4
                    pe.matmul(bank[7][:, :], (wqb, wkb)[n][:, :], xt["in"][:, :], start=True, stop=True).then_inc(m["bqkv_ps"], 1)
                    side_used("qv_ready", b * 2 + n + 1)
                if at == (6, 0):
                    side_free()
                    by_tile(bank[7], xt["in"], wvb[:, :]).then_inc(m["bqkv_ps"], 1)
                    side_used("vb_ready", b + 1)
                if at in PLACED:
                    place_rows(b, *PLACED[at])

            def heads_batch(i, finish, prepare):
                for at in ((s, half) for s in range(STEPS) for half in range(2)):
                    s, half = at
                    ahead = s + LEAD < STEPS or prepare
                    if half == 0 and (s + LEAD) % T == 0 and ahead:
                        group_placed(i, (s + LEAD) // T)
                    if half == 0 and s % T == 0:
                        pe.wait_ge(m["qpm_ready"], i * G + s // T + 1)
                        pe.wait_ge(m["va_ready"], i * G + s // T + 1)
                    for hh in (2 * half, 2 * half + 1):
                        if ahead:
                            score(i, s + LEAD, hh)
                        keys(i, s, hh)
                    if half == 0 and (s >= 1 or finish):
                        values(i, s - 1)
                    if at in ((5, 0), (9, 0), (13, 0)):
                        to_rows(i, s // T - 1)
                    if finish:
                        finish_at(i - 1, at)
                    if at in LATE:
                        place_rows(i, G - 1, half)
                    if prepare:
                        prepare_at(i + 1, at)
                    if at in ((2, 1), (6, 1), (10, 1)):
                        max_rows(i, s // T + 1)
                    if at == (14, 1) and prepare:
                        max_rows(i + 1, 0)

            if stages >= 3:
                for at in ((3, 1), (4, 1), (5, 1), (6, 0), *PLACED):
                    prepare_at(0, at)
                for k in range(LEAD):
                    if k % T == 0:
                        group_placed(0, k // T)
                    for hh in range(GH):
                        score(0, k, hh)
                max_rows(0, 0)
                heads_batch(0, False, True)
                with pe.Fori(1, B - 1) as i:
                    side_used("qpm_ready", i * G + 1)
                    heads_batch(i, True, True)
                side_used("qpm_ready", (B - 1) * G + 1)
                heads_batch(B - 1, True, False)
                values(B - 1, STEPS - 1)
                for at in ((1, 0), (3, 0), (4, 0), (8, 0), (10, 0)):
                    finish_at(B - 1, at)
            if stages >= 4:
                feed_forward(B)


_INS = ("x", "wq", "wk", "wv", "wo", "wqb", "wkb", "wvb", "wfc", "cols", "rows", "rw", "pes", "wgate", "wdown",
        "ident", "own", "block_mask", "iota", "place", "pick")


def kernel(L0_attn_a_x, L0_attn_a_Wq, L0_attn_a_bq, L0_attn_a_Wk, L0_attn_a_bk, L0_attn_a_Wv, L0_attn_a_bv, L0_attn_a_Wo,
           L0_attn_a_bo, L0_attn_b_head_mask, L0_attn_b_qkv_w, L0_attn_b_qkv_b, L0_attn_b_fc_w, L0_attn_b_fc_b,
           L0_ffn_router_scale, L0_ffn_router_w, L0_ffn_gating_w, L0_ffn_linear_w, L0_ffn_per_expert_scale, stages=4):
    import numpy as np
    import concourse.bacc as bacc
    from concourse.bass_utils import run_bass_kernel_spmd

    A = np.asarray
    qkv = A(L0_attn_b_qkv_w).reshape(H, 3, HD, P)
    qkvb = A(L0_attn_b_qkv_b).reshape(H, 3, HD)
    mask = np.repeat(A(L0_attn_b_head_mask), HD)
    p = np.arange(P)
    own = np.where(np.arange(NC)[None, None, :] == np.arange(T)[None, :, None] * T + p[:, None, None] // CHUNK, 2, 1)
    block_mask = np.broadcast_to(np.arange(T)[None, :, None] == p[:, None, None] // CHUNK, (P, T, CHUNK))
    one_rows = (p % 32 == ONE) | (p % 32 == ONE + 1)
    of_head = [p // 32 == h for h in range(GH)]
    place = np.zeros((P, 4, G, P), np.float32)
    for part, copies in enumerate(((0, 1), (2,), (0, 2), (1,))):
        for c in copies:
            for h in range(H):
                for j in range(HD):
                    place[h * HD + j, part, h // GH, h % GH * 32 + c * HD + j] = 1
    pick = np.arange(2 * NE)[:, None] % NE == np.arange(NE)[None, :]
    arrays = {
        "x": A(L0_attn_a_x).reshape(B * S, P), "wq": A(L0_attn_a_Wq), "wk": A(L0_attn_a_Wk), "wv": A(L0_attn_a_Wv), "wo": A(L0_attn_a_Wo),
        "wqb": qkv[:, 0].reshape(P, P).T, "wkb": qkv[:, 1].reshape(P, P).T, "wvb": qkv[:, 2].reshape(P, P).T,
        "wfc": A(L0_attn_b_fc_w).T,
        "cols": np.stack([A(L0_attn_a_bq), A(L0_attn_a_bk), qkvb[:, 0].reshape(P), qkvb[:, 1].reshape(P), mask,
                          A(L0_ffn_router_scale)] + [a.astype(np.float32) for a in of_head + [one_rows]], 1),
        "rows": np.stack([A(L0_attn_a_bv), A(L0_attn_a_bo), qkvb[:, 2].reshape(P), A(L0_attn_b_fc_b), mask]),
        "rw": A(L0_ffn_router_w), "pes": A(L0_ffn_per_expert_scale),
        "wgate": A(L0_ffn_gating_w).transpose(3, 1, 0, 2).reshape(P, 2 * UNITS * P),
        "wdown": A(L0_ffn_linear_w).reshape(UNITS, P, P).transpose(1, 0, 2).reshape(P, UNITS * P),
        "ident": np.eye(P, dtype=np.float32), "own": own.astype(np.float32), "block_mask": block_mask.astype(np.float32),
        "iota": np.broadcast_to(np.arange(NE, dtype=np.float32), (P, NE)), "place": place, "pick": pick.astype(np.float32),
    }
    nc = bacc.Bacc("TRN2", target_bir_lowering=False, num_devices=1)
    sent, d = {}, {}
    for name in _INS:
        a = np.ascontiguousarray(arrays[name])
        sent[f"in_{name}"] = a
        d[name] = nc.dram_tensor(f"in_{name}", a.shape, mybir.dt.from_np(a.dtype), kind="ExternalInput").ap()
    out = nc.dram_tensor("out", (B * S, P), F32, kind="ExternalOutput").ap()
    build(nc, d, out, stages)
    r = run_bass_kernel_spmd(nc, [sent], core_ids=[0])
    return r.results[0]["out"].reshape(B, S, P)
```

```python
import concourse.bass as bass
from concourse import mybir
from concourse.alu_op_type import AluOpType as ALU
from contextlib import ExitStack

ACT = mybir.ActivationFunctionType
AX = mybir.AxisListType
F32 = mybir.dt.float32
F32R = mybir.dt.float32r
U32 = mybir.dt.uint32

P = 128
B = 8
T = 4
S = P * T
CHUNK = 32
NC = S // CHUNK
H, HD = 16, 8
G = 4
GH = H // G
NE, HID = 8, 256
UNITS = NE * HID // P
ONE = 24
SCALE_A = float(P) ** -0.5
SCALE_B = float(HD) ** -0.5
AHEAD = 3
ACTS = 4
EBUFS = 4
PLACED = {(7, 0): (0, 0), (7, 1): (0, 1), (8, 1): (1, 0), (9, 1): (1, 1), (12, 0): (2, 0), (12, 1): (2, 1)}
LATE = ((0, 0), (0, 1))
KINDS = ("in", "ff")
N_EARLY, N_CONST = 6, 11

ROUTE_LINKS = 11
STEPS = G * T
LEAD = T + 2


def build(nc, d, out):
    with ExitStack() as ctx:
        def sb(name, shape, dt=F32):
            return ctx.enter_context(nc.sbuf_tensor(name, shape, dt))

        def sem(name):
            return ctx.enter_context(nc.semaphore(name))

        banks = ctx.enter_context(nc.psum_tensor("banks", [P, 8, S], F32))
        bank = [banks[:, n, :] for n in range(8)]
        KEY_BANKS = (2, 4)

        res = sb("res", [P, B * T, P])
        xcols = sb("xcols", [P, B * S])
        combt = sb("combt", [2 * NE, S], F32R)
        combc = sb("combc", [P, T, 2 * NE])
        comb16 = sb("comb16", [P, B * T, 2 * NE])

        wq, wk, wv, wo = (sb(n, [P, P]) for n in ("wq", "wk", "wv", "wo"))
        wqb, wkb, wvb, wfc = (sb(n, [P, P]) for n in ("wqb", "wkb", "wvb", "wfc"))
        cols = sb("cols", [P, 7 + GH])
        rows = sb("rows", [P, 5, P])
        rw, rws = sb("rw", [P, NE]), sb("rws", [P, NE])
        pes = sb("pes", [P, NE])
        ident = sb("ident", [P, P])
        identr = sb("identr", [P, P], F32R)
        own = sb("own", [P, T, NC])
        block_mask = sb("block_mask", [P, T, CHUNK])
        iota = sb("iota", [P, NE])
        placer = sb("placer", [P, 4, G, P], F32R)
        pick = sb("pick", [2 * NE, NE])
        pickr = sb("pickr", [2 * NE, NE], F32R)
        wstage = sb("wstage", [P, 3 * UNITS * P])
        W_PART = 3 * UNITS * P // (B - 2)
        wh, wl = sb("wh", [P, 3 * UNITS * P], F32R), sb("wl", [P, 3 * UNITS * P], F32R)

        stat = {k: sb("stat_" + k, [P, T, 6]) for k in KINDS}
        mv = {k: sb("mv_" + k, [P, T, 2]) for k in KINDS}
        rstd = {k: sb("rstd_" + k, [P, T]) for k in KINDS}
        xn = {k: sb("xn_" + k, [P, T, P]) for k in KINDS}
        xt = {k: sb("xt_" + k, [P, S]) for k in KINDS}
        rs = sb("rs", [P, T])
        consts = sb("consts", [P, 3, T])
        lg, lgn, ex8, sel, comb = (sb(n, [P, T, NE]) for n in ("lg", "lgn", "ex8", "sel", "comb"))
        sel2 = sb("sel2", [P, T, 2, NE])
        top = sb("top", [P, T, NE])
        topi = sb("topi", [P, T, NE], U32)
        topf = sb("topf", [P, T, 2])
        tot, ren, low0, rec1 = (sb(n, [P, T]) for n in ("tot", "ren", "low0", "rec1"))
        combh = sb("combh", [P, T, NE], F32R)

        qt, kt = sb("qt", [P, S]), sb("kt", [P, S])
        v = sb("v", [P, T, P])
        nmax = sb("nmax", [P, T, NC])
        tsum = sb("tsum", [P, T, NC])
        wgt = sb("wgt", [P, T, NC])
        with (nc.sbuf_tensor("shifted", [P, T, S], F32) as shifted, nc.sbuf_tensor("expd", [P, T, S], F32) as expd,
              nc.sbuf_tensor("place", [P, 4, G, P], F32) as place):
            pass
        room = sb("room", [P, 5 * T, S], F32R)
        attn = sb("attn", [P, T, CHUNK])
        abd = sb("abd", [P, T, P])
        tcol = sb("tcol", [P, S])
        ccol = sb("ccol", [P, S])

        qv, kv = qt, kt
        qh, ql = sb("qh", [P, S], F32R), sb("ql", [P, S], F32R)
        qp = room[:, 0:G, :]
        kp = room[:, G:5 * G, :].rearrange("p (h g) s -> p h g s", h=GH)
        qpm = sb("qpm", [P, 2, S], F32R)
        kh, kl = sb("kh", [P, S], F32R), sb("kl", [P, S], F32R)
        krow = sb("krow", [P, S], F32R)
        nm = sb("nm", [P, 2, T, GH])
        mpad = sb("mpad", [P, T, GH, 32], F32R)
        va = wstage[:, 2 * UNITS * P:].rearrange("p (t h c) -> p t h c", t=T, h=H)
        eb = wstage[:, 0:2 * UNITS * P].rearrange("p (n s) -> p n s", s=2 * S)
        rden = sb("rden", [P, T, GH])
        on = abd
        ov = tcol

        gel, prod = expd[:, 0:2, :], expd[:, 2:4, :]
        act = shifted
        acth, actl = room[:, 2 * T:2 * T + ACTS, :], room[:, 2 * T + ACTS:2 * T + 2 * ACTS, :]
        xh, xl = room[:, 4 * T:4 * T + 2, :], room[:, 4 * T + 2:4 * T + 4, :]
        ocol = ccol

        names = """x_loaded early_loaded w_loaded place_loaded placer_ready ffw_loaded consts_ready passed stat_in stat_ff mv_in mv_ff var_in var_ff rstd_in rstd_ff top_ready pool_link half_ready rs_ready rws_ready wh_ready wl_ready
            link nmax_ready tsum_ready tinv_ready k_ps v_ps kt_ready norm_link mpad_link lg_ready vb_ready normed xt_ps xt_ready bias_added
            q_ps qt_ready v_ready s_ps shift_done exp_done wgt_ready weighted attn_ready abd_ready abd_ps
            abdt_ready c_ps ct_ready o_ps res_a
            normed2 xt2_ps xt2_ready xcols_ready xh_ready xl_ready logit_ps lgn_ready ren_ready route_link centred_in centred_ff ex8_ready comb_ready comb_ps combt_ready
            combc_ready gates gel_done prod_done cb_ps act_done acth_done actl_done down ocol_ready ot_ps res_f
            bnormed bxt_ps bxt_ready bqkv_ps qv_ready qh_ready ql_ready va_ready krow_ready kp_ready qp_ps qp_ready
            sc_ps sc_max mpad_ready qpm_ps qpm_ready st_ps st_exp pv_done ov_ready on_ps on_ready ont_ps
            ont_ready fc_ps res_b stored zeroed ones_ready""".split()
        m = {n: sem(n) for n in names}

        block = ctx.enter_context(nc.Block())

        def tile(i, t):
            return res[:, bass.ds(i * T + t, 1), :].rearrange("p a d -> p (a d)")

        def batch(i):
            return res[:, bass.ds(i * T, T), :]

        def at_first(i):
            return isinstance(i, int) and i == 0

        def over_batches(engine, first, body, beside_first, beside_last):
            body(first, 0, 0, False, True, beside_first)
            with engine.Fori(0, (B - 2) // 2) as j:
                for k in range(2):
                    i = j * 2 + 1 + k
                    body(i + first, i, 1 - k, True, True, None)
            body(first + B - 1, B - 1, 1, True, False, beside_last)

        def besides(first, after_chunks, before_heads, after_heads):
            if first == 0:
                return after_chunks, before_heads
            return after_heads, None

        def over_tiles(ap2):
            return ap2.unsqueeze(1).to_broadcast([P, T, P])

        @block.sync
        def _(sp):
            x_rows = d["x"].rearrange("(b t p) e -> b p t e", t=T, p=P)
            sp.dma_start(batch(0), x_rows[0]).then_inc(m["x_loaded"], 16)
            sp.dma_start(own[:, :, :], d["own"]).then_inc(m["w_loaded"], 16)
            sp.dma_start(block_mask[:, :, :], d["block_mask"]).then_inc(m["w_loaded"], 16)
            sp.dma_start(pes[:, :], d["pes"].unsqueeze(0).to_broadcast([P, NE])).then_inc(m["w_loaded"], 16)
            for dst, name in ((rw, "rw"), (wo, "wo"), (iota, "iota"), (pick, "pick"),
                              (wqb, "wqb"), (wkb, "wkb"), (wvb, "wvb"), (wfc, "wfc")):
                sp.dma_start(dst[:, :], d[name]).then_inc(m["w_loaded"], 16)

            def load(i):
                sp.wait_ge(m["x_loaded"], i * 16)
                sp.dma_start(batch(i), x_rows[bass.ds(i, 1)].rearrange("b p t e -> p (b t) e")).then_inc(m["x_loaded"], 16)

            load(1)
            sp.dma_start(wstage[:, 0:2 * UNITS * P], d["wgate"]).then_inc(m["ffw_loaded"], 16)
            sp.dma_start(wstage[:, 2 * UNITS * P:], d["wdown"]).then_inc(m["ffw_loaded"], 16)
            sp.dma_start(place[:, :, :, :], d["place"]).then_inc(m["place_loaded"], 16)
            with sp.Fori(2, B) as i:
                load(i)
            o_rows = out.rearrange("(b t p) e -> b p t e", t=T, p=P)
            with sp.Fori(0, B) as i:
                sp.wait_ge(m["res_f"], B + i + 1)
                sp.dma_start(o_rows[bass.ds(i, 1)].rearrange("b p t e -> p (b t) e"), batch(i)).then_inc(m["stored"], 16)
            sp.wait_ge(m["stored"], 16 * B)

        @block.vector
        def _(dve):
            def statistics(i, n, kind):
                dve.sem_inc(m["passed"], 1)
                for t in range(T):
                    last = dve.bn_stats(stat[kind][:, t, :], tile(i, t))
                last.then_inc(m["stat_" + kind], 1)
                dve.wait_ge(m["stat_" + kind], n + 1)
                dve.sem_inc(m["passed"], 1)
                for t in range(T):
                    last = dve.bn_aggr(mv[kind][:, t, :], stat[kind][:, t, :])
                last.then_inc(m["mv_" + kind], 1)

            def normalised(i, n, kind, done):
                dve.wait_ge(m["rstd_" + kind], n + 1)
                for t in range(T):
                    last = dve.tensor_scalar(xn[kind][:, t, :], tile(i, t), mv[kind][:, t, 0:1], rstd[kind][:, t:t + 1],
                                             ALU.subtract, ALU.mult)
                last.then_inc(m[done], 1)

            def chain(n, done):
                k = [done]

                def link(ins):
                    ins.then_inc(m["link"], 1)
                    k[0] += 1
                    dve.wait_ge(m["link"], n * ROUTE_LINKS + k[0])
                return link, k

            def route_logits(n, products):
                dve.wait_ge(m["rs_ready"], n + 1)
                dve.wait_ge(m["logit_ps"], n + 1)
                dve.tensor_tensor(lg[:, :, :], products[:, 0:T * NE].rearrange("p (t e) -> p t e", e=NE),
                                  rs[:, :].unsqueeze(2).to_broadcast([P, T, NE]), ALU.mult).then_inc(m["lg_ready"], 1)
                dve.wait_ge(m["lg_ready"], n + 1)
                dve.sem_inc(m["passed"], 1)
                for t in range(T):
                    last = dve.max(top[:, t, :], lg[:, t, :])
                last.then_inc(m["top_ready"], 1)
                dve.wait_ge(m["top_ready"], n + 1)
                dve.tensor_tensor(lgn[:, :, :], lg[:, :, :], top[:, :, 0:1].to_broadcast([P, T, NE]),
                                  ALU.subtract).then_inc(m["lgn_ready"], 1)

            def route_choice(n):
                link, k = chain(n, 0)
                for t in range(T):
                    last = dve.max_index(topi[:, t, :], top[:, t, :], lg[:, t, :])
                link(last)
                link(dve.tensor_copy(topf[:, :, :], topi[:, :, 0:2]))
                link(dve.tensor_tensor(sel2[:, :, :, :], iota[:, :].unsqueeze(1).unsqueeze(1).to_broadcast([P, T, 2, NE]),
                                       topf[:, :, :].unsqueeze(3).to_broadcast([P, T, 2, NE]), ALU.is_equal))
                link(dve.tensor_tensor(sel[:, :, :], sel2[:, :, 0, :], sel2[:, :, 1, :], ALU.add))
                assert k[0] == 4, k[0]

            def route_softmax(n):
                link, k = chain(n, 4)
                dve.wait_ge(m["ex8_ready"], n + 1)
                link(dve.tensor_reduce(tot[:, :], ex8[:, :, :], AX.X, ALU.add))
                if not at_first(n):
                    dve.wait_ge(m["comb_ready"], n)
                link(dve.reciprocal(rec1[:, :], tot[:, :]))
                link(dve.tensor_tensor(comb[:, :, :], ex8[:, :, :], rec1[:, :].unsqueeze(2).to_broadcast([P, T, NE]), ALU.mult))
                link(dve.tensor_tensor(comb[:, :, :], comb[:, :, :], sel[:, :, :], ALU.mult))
                link(dve.tensor_reduce(ren[:, :], comb[:, :, :], AX.X, ALU.add))
                link(dve.tensor_scalar(low0[:, :], ren[:, :], 0.0, None, ALU.is_le))
                link(dve.tensor_tensor(ren[:, :], ren[:, :], low0[:, :], ALU.max))
                assert k[0] == ROUTE_LINKS, k[0]
                dve.reciprocal(rec1[:, :], ren[:, :]).then_inc(m["ren_ready"], 1)

            def constants():
                dve.wait_ge(m["early_loaded"], 16 * N_EARLY)
                dve.wait_ge(m["w_loaded"], 16 * N_CONST)
                dve.tensor_copy(identr[:, :], ident[:, :])
                dve.tensor_copy(pickr[:, :], pick[:, :])
                dve.memset(mpad[:, :, :, :].rearrange("p t h c -> p (t h c)").bitcast(F32), 0.0).then_inc(m["consts_ready"], 1)
                dve.tensor_scalar(rws[:, :], rw[:, :], cols[:, 5:6], SCALE_A, ALU.mult, ALU.mult).then_inc(m["rws_ready"], 1)

            def scores_shifted(i, t):
                dve.wait_ge(m["s_ps"], i * T + t + 1)
                scores = bank[4 + t][:, :].rearrange("p (m k) -> p m k", k=CHUNK)
                dve.tensor_reduce(nmax[:, t, :], scores, AX.X, ALU.max, negate=True).then_inc(m["nmax_ready"], 1)
                dve.wait_ge(m["nmax_ready"], i * T + t + 1)
                dve.tensor_tensor(shifted[:, t, :].rearrange("p (m k) -> p m k", k=CHUNK), scores,
                                  nmax[:, t, :].unsqueeze(2).to_broadcast([P, NC, CHUNK]), ALU.add).then_inc(m["shift_done"], 1)

            def chunk_weights(i, t):
                dve.wait_ge(m["exp_done"], i * T + t + 1)
                dve.tensor_reduce(tsum[:, t, :], expd[:, t, :].rearrange("p (m k) -> p m k", k=CHUNK), AX.X, ALU.add).then_inc(m["tsum_ready"], 1)
                dve.wait_ge(m["tsum_ready"], i * T + t + 1)
                dve.reciprocal(tsum[:, t, :], tsum[:, t, :]).then_inc(m["tinv_ready"], 1)
                dve.wait_ge(m["tinv_ready"], i * T + t + 1)
                dve.tensor_tensor(wgt[:, t, :], tsum[:, t, :], own[:, t, :], ALU.mult).then_inc(m["wgt_ready"], 1)

            def chunks_summed(i, t):
                dve.wait_ge(m["weighted"], i * T + t + 1)
                dve.tensor_reduce(attn[:, t, :], shifted[:, t, :].rearrange("p (m k) -> p k m", k=CHUNK), AX.X,
                                  ALU.add).then_inc(m["attn_ready"], 1)

            def values_biased(i):
                dve.wait_ge(m["v_ps"], i + 1)
                dve.tensor_tensor(v[:, :, :], bank[1][:, :].rearrange("p (t e) -> p t e", e=P), over_tiles(rows[:, 0, :]),
                                  ALU.add).then_inc(m["v_ready"], 1)

            def chunks_out(i, to=bank[2]):
                dve.wait_ge(m["o_ps"], i + 1)
                dve.wait_ge(m["bias_added"], i + 1)
                dve.tensor_tensor(batch(i), batch(i), to[:, :].rearrange("p (t e) -> p t e", e=P),
                                  ALU.add).then_inc(m["res_a"], 1)
                dve.wait_ge(m["res_a"], i + 1)
                statistics(i, i, "ff")

            def chunks_batch(i, before, after):
                if after:
                    dve.wait_ge(m["x_loaded"], i * 16 + 32)
                    statistics(i + 1, i + 1, "in")
                scores_shifted(i, 0)
                if after:
                    normalised(i + 1, i + 1, "in", "normed")
                scores_shifted(i, 1)
                chunk_weights(i, 0)
                scores_shifted(i, 2)
                values_biased(i)
                if before:
                    chunks_out(i - 1)
                chunk_weights(i, 1)
                if before:
                    normalised(i - 1, i - 1, "ff", "normed2")
                scores_shifted(i, 3)
                chunk_weights(i, 2)
                chunks_summed(i, 0)
                chunk_weights(i, 3)
                chunks_summed(i, 1)
                if before:
                    route_logits(i - 1, bank[2])
                    route_choice(i - 1)
                chunks_summed(i, 2)
                if before:
                    route_softmax(i - 1)
                chunks_summed(i, 3)

            dve.wait_ge(m["x_loaded"], 16)
            statistics(0, 0, "in")
            normalised(0, 0, "in", "normed")
            constants()
            chunks_batch(0, False, True)
            with dve.Fori(1, B - 1) as i:
                chunks_batch(i, True, True)
            chunks_batch(B - 1, True, False)

            def chunks_beside(u):
                if u == 4:
                    chunks_out(B - 1, bank[7])
                if u == 7:
                    normalised(B - 1, B - 1, "ff", "normed2")
                if u == 10:
                    route_logits(B - 1, bank[7])
                if u == 11:
                    route_choice(B - 1)
                if u == 12:
                    route_softmax(B - 1)
                if u == 14:
                    dve.wait_ge(m["wl_ready"], B - 2)
                    dve.memset(wstage[:, 2 * UNITS * P:], 0.0).then_inc(m["zeroed"], 1)
                if u == 15:
                    dve.wait_ge(m["zeroed"], 1)
                    dve.memset(va[:, :, :, HD:HD + 1], 1.0).then_inc(m["ones_ready"], 1)

            def ff_batch(n, i, parity, before, after, beside):
                for u in range(UNITS):
                    dve.wait_ge(m["gel_done"], n * UNITS + u + 1)
                    dve.tensor_tensor(prod[:, u % 2, :], bank[2 + u % 2][:, :], gel[:, u % 2, :], ALU.mult).then_inc(m["prod_done"], 1)
                    if u % 2 == 0:
                        dve.wait_ge(m["cb_ps"], n * NE + u // 2 + 1)
                    dve.wait_ge(m["prod_done"], n * UNITS + u + 1)
                    if u >= ACTS or before:
                        dve.wait_ge(m["actl_done"], n * UNITS + u - ACTS + 1)
                    dve.tensor_tensor(act[:, u % ACTS, :], bank[4 + (u // 2) % 2][:, :], prod[:, u % 2, :], ALU.mult).then_inc(m["act_done"], 1)
                    if u == AHEAD + 2 and before:
                        ff_out(n - 1, i - 1)
                    if beside:
                        beside(u)

            def ff_out(n, i):
                dve.wait_ge(m["ot_ps"], n + 1)
                dve.tensor_tensor(batch(i), batch(i), bank[7][:, :].rearrange("p (t e) -> p t e", e=P),
                                  ALU.add).then_inc(m["res_f"], 1)

            def feed_forward(first):
                over_batches(dve, first, ff_batch, *besides(first, chunks_beside, heads_ahead, heads_beside))
                ff_out(first + B - 1, B - 1)
            def maxima(i, at, half):
                for hh in (2 * half, 2 * half + 1):
                    n = i * (H * T) + at * GH + hh
                    dve.wait_ge(m["sc_ps"], n + 1)
                    dve.tensor_reduce(nm[:, at // T % 2, at % T, hh:hh + 1], bank[hh % 2][:, :], AX.X, ALU.max, negate=True).then_inc(m["sc_max"], 1)

            def maxima_rows(b, g):
                dve.wait_ge(m["sc_max"], b * (H * T) + (g + 1) * T * GH)
                if not (at_first(b) and g == 0):
                    dve.wait_ge(m["qpm_ps"], b * G + g)
                    dve.wait_ge(m["mpad_ready"], b * G + g)
                dve.tensor_copy(mpad[:, :, :, ONE], nm[:, g % 2, :, :]).then_inc(m["mpad_link"], 1)
                dve.wait_ge(m["mpad_link"], b * G + g + 1)
                dve.tensor_tensor(mpad[:, :, :, ONE + 1], nm[:, g % 2, :, :], mpad[:, :, :, ONE], ALU.subtract).then_inc(m["mpad_ready"], 1)

            def normalise(b, g):
                dve.wait_ge(m["on_ps"], b * G + g + 1)
                sums = bank[7][:, :].rearrange("p (t h c) -> p t h c", h=GH, c=32)
                dve.reciprocal(rden[:, :, :], sums[:, :, :, HD]).then_inc(m["norm_link"], 1)
                dve.wait_ge(m["norm_link"], b * G + g + 1)
                dve.tensor_tensor(on[:, :, g * 32:g * 32 + 32].rearrange("p t (h j) -> p t h j", j=HD), sums[:, :, :, 0:HD],
                                  rden[:, :, :].unsqueeze(3).to_broadcast([P, T, GH, HD]), ALU.mult).then_inc(m["on_ready"], 1)

            def head_rows(b, n, bias):
                dve.wait_ge(m["bqkv_ps"], b * 3 + n + 1)
                dve.tensor_scalar((qv, kv)[n][:, :], bank[7][:, :], cols[:, bias:bias + 1], cols[:, 4:5], ALU.add, ALU.mult).then_inc(m["qv_ready"], 1)

            def values_in(b):
                if not at_first(b):
                    dve.wait_ge(m["va_ready"], b * G)
                dve.wait_ge(m["bqkv_ps"], b * 3 + 3)
                dve.tensor_tensor(v[:, :, :], bank[7][:, :].rearrange("p (t e) -> p t e", e=P), over_tiles(rows[:, 2, :]), ALU.add).then_inc(m["vb_ready"], 1)

            def heads_out(b):
                dve.wait_ge(m["fc_ps"], b + 1)
                dve.wait_ge(m["bias_added"], B + b + 1)
                dve.tensor_tensor(batch(b), batch(b), bank[7][:, :].rearrange("p (t e) -> p t e", e=P), ALU.add).then_inc(m["res_b"], 1)

            def finish_at(b, at, prepared=False):
                if at == (1, 0):
                    normalise(b, G - 1)
                if at == (4, 0):
                    heads_out(b)
                if at == (5, 0):
                    dve.wait_ge(m["res_b"], b + 1)
                    dve.wait_ge(m["normed2"], b + B)
                    statistics(b, b + B, "ff")
                if at == (11, 0):
                    route_logits(b + B, bank[7])
                if at == (12, 0):
                    route_choice(b + B)
                if at == (14, 0):
                    route_softmax(b + B)

            def prepare_at(b, at):
                if at == (0, 1):
                    if not at_first(b):
                        dve.wait_ge(m["bnormed"], b)
                    statistics(b, b + B, "in")
                if at == (4, 1):
                    head_rows(b, 0, 2)
                if at == (5, 1):
                    head_rows(b, 1, 3)
                if at == (6, 0):
                    values_in(b)

            def heads_batch(i, finish, prepare):
                for at in ((s, half) for s in range(STEPS) for half in range(2)):
                    s, half = at
                    if s + LEAD < STEPS or prepare:
                        maxima(i, s + LEAD, half)
                    if at in ((5, 0), (9, 0), (13, 0)):
                        normalise(i, s // T - 1)
                    if finish:
                        finish_at(i - 1, at, prepare)
                    if prepare:
                        prepare_at(i + 1, at)
                    if at in ((1, 1), (5, 1), (9, 1)):
                        maxima_rows(i, s // T + 1)
                    if at == (13, 1) and prepare:
                        maxima_rows(i + 1, 0)

            def heads_ahead(u):
                if u in (1, 7, 8, 9):
                    prepare_at(0, {1: (0, 1), 7: (4, 1), 8: (5, 1), 9: (6, 0)}[u])

            def heads_beside(u):
                if u in (1, 6, 10, 11, 13):
                    finish_at(B - 1, {1: (1, 0), 6: (4, 0), 10: (11, 0), 11: (12, 0), 13: (14, 0)}[u])
                if u == 6:
                    finish_at(B - 1, (5, 0))

            feed_forward(0)
            for k in range(LEAD):
                for half in range(2):
                    maxima(0, k, half)
                if k == T - 1:
                    maxima_rows(0, 0)
            heads_batch(0, False, True)
            with dve.Fori(1, B - 1) as i:
                heads_batch(i, True, True)
            heads_batch(B - 1, True, False)
            feed_forward(B)

        @block.scalar
        def _(act_e):
            for dst, name in ((ident, "ident"), (wq, "wq"), (cols, "cols"), (wk, "wk"), (wv, "wv")):
                act_e.dma_start(dst[:, :], d[name]).then_inc(m["early_loaded"], 16)
            act_e.dma_start(rows[:, :, :], d["rows"].unsqueeze(0).to_broadcast([P, 5, P])).then_inc(m["early_loaded"], 16)

            def copy(dst, src):
                return act_e.activation(dst, src, ACT.Copy)

            def routed_columns(i, n, side):
                act_e.wait_ge(m["xt2_ps"], n + 1)
                copy(xt["ff"][:, :], side).then_inc(m["xt2_ready"], 1)
                copy(xcols[:, bass.ds(i * S, S)], side).then_inc(m["xcols_ready"], 1)

            def routed_exponentials(n):
                act_e.wait_ge(m["lgn_ready"], n + 1)
                act_e.activation(ex8[:, :, :], lgn[:, :, :], ACT.Exp).then_inc(m["ex8_ready"], 1)

            def chunks_columns(i):
                act_e.wait_ge(m["xt_ps"], i + 1)
                copy(xt["in"][:, :], bank[0][:, :]).then_inc(m["xt_ready"], 1)

            def chunks_queries(i):
                act_e.wait_ge(m["q_ps"], i + 1)
                act_e.activation(qt[:, :], bank[1][:, :], ACT.Identity, bias=cols[:, 0:1]).then_inc(m["qt_ready"], 1)

            def chunks_keys(i):
                act_e.wait_ge(m["k_ps"], i + 1)
                act_e.activation(kt[:, :], bank[0][:, :], ACT.Identity, bias=cols[:, 1:2]).then_inc(m["kt_ready"], 1)

            def chunks_exponentials(i, t):
                act_e.wait_ge(m["shift_done"], i * T + t + 1)
                act_e.activation(expd[:, t, :], shifted[:, t, :], ACT.Exp, scale=SCALE_A).then_inc(m["exp_done"], 1)

            def attention_columns(i, to=bank[2]):
                act_e.wait_ge(m["abd_ps"], i + 1)
                copy(tcol[:, :], to[:, :]).then_inc(m["abdt_ready"], 1)

            def combined_columns(i, to=bank[3]):
                act_e.wait_ge(m["c_ps"], i + 1)
                copy(ccol[:, :], to[:, :]).then_inc(m["ct_ready"], 1)

            def chunks_batch(i, before, after):
                if before:
                    attention_columns(i - 1)
                chunks_exponentials(i, 0)
                if before:
                    combined_columns(i - 1)
                chunks_exponentials(i, 1)
                if after:
                    chunks_columns(i + 1)
                if after:
                    chunks_queries(i + 1)
                chunks_exponentials(i, 2)
                if after:
                    chunks_keys(i + 1)
                chunks_exponentials(i, 3)
                if before:
                    routed_columns(i - 1, i - 1, bank[3][:, :])
                    routed_exponentials(i - 1)

            act_e.wait_ge(m["early_loaded"], 16 * N_EARLY)
            chunks_columns(0)
            chunks_queries(0)
            chunks_keys(0)
            chunks_batch(0, False, True)
            act_e.wait_ge(m["ffw_loaded"], 32)
            with act_e.Fori(1, B - 1) as i:
                part = bass.ds((i - 1) * W_PART, W_PART)
                copy(wh[:, part], wstage[:, part]).then_inc(m["wh_ready"], 1)
                chunks_batch(i, True, True)
            act_e.wait_ge(m["place_loaded"], 16)
            copy(placer[:, :, :, :], place[:, :, :, :]).then_inc(m["placer_ready"], 1)
            chunks_batch(B - 1, True, False)

            def chunks_beside(u):
                if u == 0:
                    attention_columns(B - 1, bank[7])
                if u == 2:
                    combined_columns(B - 1, bank[7])
                if u == 8:
                    routed_columns(B - 1, B - 1, bank[7][:, :])
                if u == 11:
                    routed_exponentials(B - 1)

            def ff_columns(n, i, parity):
                act_e.wait_ge(m["xcols_ready"], n + 1)
                copy(xh[:, parity, :], xcols[:, bass.ds(i * S, S)]).then_inc(m["xh_ready"], 1)

            def ff_weights(n, i):
                act_e.wait_ge(m["comb_ready"], n + 1)
                copy(combc[:, :, :], comb16[:, bass.ds(i * T, T), :]).then_inc(m["combc_ready"], 1)

            def ff_weight_columns(n):
                act_e.wait_ge(m["comb_ps"], n + 1)
                copy(combt[:, :], bank[7][0:2 * NE, :]).then_inc(m["combt_ready"], 1)

            def ff_high(n, u):
                act_e.wait_ge(m["act_done"], n * UNITS + u + 1)
                copy(acth[:, u % ACTS, :], act[:, u % ACTS, :]).then_inc(m["acth_done"], 1)

            def ff_out(n):
                act_e.wait_ge(m["down"], n * UNITS)
                copy(ocol[:, :], bank[6][:, :]).then_inc(m["ocol_ready"], 1)

            def ff_batch(n, i, parity, before, after, beside):
                for u in range(UNITS):
                    if u == AHEAD and before:
                        ff_out(n)
                    act_e.wait_ge(m["gates"], n * UNITS + u + 1)
                    act_e.activation(gel[:, u % 2, :], bank[u % 2][:, :], ACT.Gelu_apprx_tanh).then_inc(m["gel_done"], 1)
                    if u >= 1 or before:
                        if u > ACTS or before:
                            act_e.wait_ge(m["down"], n * UNITS + u - ACTS)
                        ff_high(n, u - 1) if u else ff_high(n - 1, UNITS - 1)
                    if after and u == 8:
                        ff_columns(n + 1, i + 1, 1 - parity)
                    if after and u == 9:
                        ff_weights(n + 1, i + 1)
                    if beside:
                        beside(u)
                if after:
                    act_e.wait_ge(m["cb_ps"], (n + 1) * NE)
                    ff_weight_columns(n + 1)

            def feed_forward(first):
                ff_columns(first, 0, 0)
                ff_weights(first, 0)
                ff_weight_columns(first)
                if first == 0:
                    act_e.wait_ge(m["weighted"], B * T)
                over_batches(act_e, first, ff_batch, *besides(first, chunks_beside, heads_ahead, heads_beside))
                ff_high(first + B - 1, UNITS - 1)
                ff_out(first + B)
            def placed(b, g, part):
                act_e.wait_ge(m["qp_ps"], b * 2 * G + 2 * g + part + 1)
                if part == 0:
                    copy(qp[:, g, :], bank[7][:, :]).then_inc(m["qp_ready"], 1)
                else:
                    if not (at_first(b) and g == 0):
                        act_e.wait_ge(m["kp_ready"], (b * G + g) * GH)
                    act_e.activation(krow[:, :], bank[7][:, :], ACT.Identity, bias=cols[:, 6 + GH:7 + GH]).then_inc(m["krow_ready"], 1)

            def exponentials(i, s, pair):
                gs = i * STEPS + s
                n = 2 * s + pair
                act_e.wait_ge(m["st_ps"], gs * 2 + pair + 1)
                if not (at_first(i) and n < EBUFS):
                    act_e.wait_ge(m["pv_done"], gs + (pair - EBUFS) // 2 + 1)
                two = KEY_BANKS[pair]
                act_e.activation(eb[:, n % EBUFS, :], banks[:, two:two + 2, :].rearrange("p a s -> p (a s)"),
                                 ACT.Exp, scale=SCALE_B).then_inc(m["st_exp"], 1)

            def maxima_in(b, g):
                act_e.wait_ge(m["qpm_ps"], b * G + g + 1)
                copy(qpm[:, g % 2, :], bank[7][:, :]).then_inc(m["qpm_ready"], 1)

            def sums_out(b, g):
                act_e.wait_ge(m["pv_done"], b * (G * T) + (g + 1) * T)
                copy(ov[:, :], bank[6][:, :]).then_inc(m["ov_ready"], 1)

            def finish_at(b, at):
                if at == (0, 0):
                    sums_out(b, G - 1)
                if at == (3, 0):
                    act_e.wait_ge(m["ont_ps"], b + 1)
                    copy(ccol[:, :], bank[7][:, :]).then_inc(m["ont_ready"], 1)
                if at == (10, 0):
                    routed_columns(b, b + B, bank[7][:, :])
                if at == (12, 0):
                    routed_exponentials(b + B)

            def prepare_at(b, at):
                if at == (3, 1):
                    act_e.wait_ge(m["bxt_ps"], b + 1)
                    copy(xt["in"][:, :], bank[7][:, :]).then_inc(m["bxt_ready"], 1)
                if at == (5, 0):
                    act_e.wait_ge(m["qv_ready"], b * 2 + 1)
                    copy(qh[:, :], qv[:, :]).then_inc(m["qh_ready"], 1)
                if at == (6, 0):
                    act_e.wait_ge(m["qv_ready"], b * 2 + 2)
                    copy(kh[:, :], kv[:, :]).then_inc(m["qh_ready"], 1)
                if at in PLACED:
                    placed(b, *PLACED[at])

            def heads_batch(i, finish, prepare):
                for at in ((s, half) for s in range(STEPS) for half in range(2)):
                    s, half = at
                    exponentials(i, s, half)
                    if at in ((4, 0), (8, 0), (12, 0)):
                        sums_out(i, s // T - 1)
                    if finish:
                        finish_at(i - 1, at)
                    if at in LATE:
                        placed(i, G - 1, half)
                    if prepare:
                        prepare_at(i + 1, at)
                    if at in ((2, 1), (6, 1), (10, 1)):
                        maxima_in(i, s // T + 1)
                    if at == (14, 1) and prepare:
                        maxima_in(i + 1, 0)

            def heads_ahead(u):
                if u in (6, 8, 9):
                    prepare_at(0, {6: (3, 1), 8: (5, 0), 9: (6, 0)}[u])

            def heads_beside(u):
                if u in (3, 9, 11):
                    finish_at(B - 1, {3: (3, 0), 9: (10, 0), 11: (12, 0)}[u])

            feed_forward(0)
            for at in PLACED:
                prepare_at(0, at)
            maxima_in(0, 0)
            heads_batch(0, False, True)
            with act_e.Fori(1, B - 1) as i:
                heads_batch(i, True, True)
            heads_batch(B - 1, True, False)
            finish_at(B - 1, (0, 0))
            feed_forward(B)

        @block.gpsimd
        def _(pool):
            for n, value in enumerate((-0.5, 1e-5, 1e-6)):
                pool.memset(consts[:, n, :], value).then_inc(m["half_ready"], 1)
            pool.wait_ge(m["half_ready"], 3)

            def deviation(n, kind):
                pool.wait_ge(m["mv_" + kind], n + 1)
                pool.tensor_tensor(rstd[kind][:, :], mv[kind][:, :, 1], consts[:, 1, :], ALU.add).then_inc(m["var_" + kind], 1)
                pool.wait_ge(m["var_" + kind], n + 1)
                pool.tensor_tensor(rstd[kind][:, :], rstd[kind][:, :], consts[:, 0, :], ALU.pow).then_inc(m["rstd_" + kind], 1)

            def route_deviation(n):
                deviation(n, "ff")
                pool.wait_ge(m["rstd_ff"], n + 1)
                for k, (in0, in1, op) in enumerate(((rstd["ff"][:, :], rstd["ff"][:, :], ALU.mult), (rs[:, :], mv["ff"][:, :, 1], ALU.mult),
                                                    (rs[:, :], consts[:, 2, :], ALU.add))):
                    pool.tensor_tensor(rs[:, :], in0, in1, op).then_inc(m["pool_link"], 1)
                    pool.wait_ge(m["pool_link"], n * 3 + k + 1)
                pool.tensor_tensor(rs[:, :], rs[:, :], consts[:, 0, :], ALU.pow).then_inc(m["rs_ready"], 1)

            def normalised(b, kind, read, done):
                pool.wait_ge(m["rstd_" + kind], b + B + 1)
                if read:
                    pool.wait_ge(m[read[0]], read[1])
                pool.sem_inc(m["passed"], 1)
                rows_in, to = batch(b), xn[kind][:, :, :]
                pool.tensor_tensor(to, rows_in, mv[kind][:, :, 0:1].to_broadcast([P, T, P]), ALU.subtract).then_inc(m["centred_" + kind], 1)
                pool.wait_ge(m["centred_" + kind], b + 1)
                pool.tensor_tensor(to, to, rstd[kind][:, :].unsqueeze(2).to_broadcast([P, T, P]), ALU.mult).then_inc(m[done], 1)

            def route_link(n, k, ins):
                ins.then_inc(m["route_link"], 1)
                pool.wait_ge(m["route_link"], n * 3 + k)

            def scaled(i, n):
                pool.wait_ge(m["ren_ready"], n + 1)
                route_link(n, 1, pool.tensor_tensor(comb[:, :, :], comb[:, :, :], rec1[:, :].unsqueeze(2).to_broadcast([P, T, NE]), ALU.mult))
                route_link(n, 2, pool.tensor_tensor(comb[:, :, :], comb[:, :, :], pes[:, :].unsqueeze(1).to_broadcast([P, T, NE]), ALU.mult))
                pool.sem_inc(m["passed"], 1)
                route_link(n, 3, pool.tensor_copy(combh[:, :, :], comb[:, :, :]))
                pool.sem_inc(m["passed"], 1)
                pool.tensor_copy(comb16[:, bass.ds(i * T, T), 0:NE], combh[:, :, :])
                pool.tensor_tensor(comb16[:, bass.ds(i * T, T), NE:2 * NE], comb[:, :, :], combh[:, :, :], ALU.subtract).then_inc(m["comb_ready"], 1)

            def bias_added(i):
                pool.wait_ge(m["normed"], i + 1)
                pool.tensor_tensor(batch(i), batch(i), over_tiles(rows[:, 1, :]), ALU.add).then_inc(m["bias_added"], 1)

            def weighted(i, t):
                pool.wait_ge(m["wgt_ready"], i * T + t + 1)
                pool.tensor_tensor(shifted[:, t, :].rearrange("p (m k) -> p m k", k=CHUNK),
                                   expd[:, t, :].rearrange("p (m k) -> p m k", k=CHUNK),
                                   wgt[:, t, :].unsqueeze(2).to_broadcast([P, NC, CHUNK]), ALU.mult).then_inc(m["weighted"], 1)

            def block_diagonal(i, t):
                pool.wait_ge(m["attn_ready"], i * T + t + 1)
                pool.tensor_tensor(abd[:, t, :].rearrange("p (c k) -> p c k", k=CHUNK), block_mask[:, :, :],
                                   attn[:, t, :].unsqueeze(1).to_broadcast([P, T, CHUNK]), ALU.mult).then_inc(m["abd_ready"], 1)

            def chunks_batch(i, before, after):
                if after:
                    deviation(i + 1, "in")
                if before and after:
                    weights_split(i)
                weighted(i, 0)
                if after:
                    bias_added(i + 1)
                if before:
                    route_deviation(i - 1)
                weighted(i, 1)
                weighted(i, 2)
                block_diagonal(i, 0)
                weighted(i, 3)
                block_diagonal(i, 1)
                block_diagonal(i, 2)
                block_diagonal(i, 3)
                if before:
                    scaled(i - 1, i - 1)

            deviation(0, "in")
            pool.wait_ge(m["early_loaded"], 16 * N_EARLY)
            bias_added(0)
            pool.wait_ge(m["w_loaded"], 16 * N_CONST)

            def weights_split(i):
                pool.wait_ge(m["wh_ready"], i)
                pool.sem_inc(m["passed"], 1)
                part = bass.ds((i - 1) * W_PART, W_PART)
                pool.tensor_tensor(wl[:, part], wstage[:, part], wh[:, part], ALU.subtract).then_inc(m["wl_ready"], 1)

            chunks_batch(0, False, True)
            with pool.Fori(1, B - 1) as i:
                chunks_batch(i, True, True)
            chunks_batch(B - 1, True, False)

            def chunks_beside(u):
                if u == 5:
                    route_deviation(B - 1)
                if u == 13:
                    scaled(B - 1, B - 1)

            def ff_columns(n, i, parity):
                pool.wait_ge(m["xh_ready"], n + 1)
                pool.tensor_tensor(xl[:, parity, :], xcols[:, bass.ds(i * S, S)], xh[:, parity, :], ALU.subtract).then_inc(m["xl_ready"], 1)

            def ff_batch(n, i, parity, before, after, beside):
                for u in range(UNITS):
                    pool.wait_ge(m["acth_done"], n * UNITS + u + 1)
                    pool.tensor_tensor(actl[:, u % ACTS, :], act[:, u % ACTS, :], acth[:, u % ACTS, :],
                                       ALU.subtract).then_inc(m["actl_done"], 1)
                    if after and u == 8:
                        ff_columns(n + 1, i + 1, 1 - parity)
                    if beside:
                        beside(u)

            def feed_forward(first):
                ff_columns(first, 0, 0)
                over_batches(pool, first, ff_batch, *besides(first, chunks_beside, heads_ahead, heads_beside))
            def heads_normalised(b):
                deviation(b + B, "in")
                normalised(b, "in", None if at_first(b) else ("bxt_ps", b), "bnormed")

            def heads_bias(b):
                pool.wait_ge(m["bnormed"], b + 1)
                pool.sem_inc(m["passed"], 1)
                pool.tensor_tensor(batch(b), batch(b), over_tiles(rows[:, 3, :]), ALU.add).then_inc(m["bias_added"], 1)

            def split(b):
                pool.wait_ge(m["qh_ready"], b * 2 + 1)
                pool.tensor_tensor(ql[:, :], qv[:, :], qh[:, :], ALU.subtract).then_inc(m["ql_ready"], 1)
                pool.wait_ge(m["qh_ready"], b * 2 + 2)
                pool.tensor_tensor(kl[:, :], kv[:, :], kh[:, :], ALU.subtract).then_inc(m["ql_ready"], 1)

            def placed(b, g):
                pool.wait_ge(m["krow_ready"], b * G + g + 1)
                for hh in range(GH):
                    pool.tensor_tensor(kp[:, hh, g, :], krow[:, :], cols[:, 6 + hh:7 + hh].to_broadcast([P, S]), ALU.mult).then_inc(m["kp_ready"], 1)
                pool.wait_ge(m["vb_ready"], b + 1)
                if not at_first(b):
                    pool.wait_ge(m["pv_done"], b * (G * T) - (G - 1 - g) * T)
                heads = slice(g * GH, (g + 1) * GH)
                pool.tensor_tensor(va[:, :, heads, 0:HD], v[:, :, g * 32:g * 32 + 32].rearrange("p t (h j) -> p t h j", j=HD),
                                   rows[:, 4, g * 32:g * 32 + 32].rearrange("p (h j) -> p h j", j=HD).unsqueeze(1).to_broadcast([P, T, GH, HD]),
                                   ALU.mult).then_inc(m["va_ready"], 1)

            def finish_normalised(b):
                route_deviation(b + B)
                normalised(b, "ff", ("xt2_ps", b + B), "normed2")

            def heads_batch(i, finish, prepare):
                if prepare:
                    heads_normalised(i + 1)
                placed(i, G - 1)
                if prepare:
                    heads_bias(i + 1)
                if finish:
                    finish_normalised(i - 1)
                if prepare:
                    split(i + 1)
                    placed(i + 1, 0)
                    placed(i + 1, 1)
                if prepare:
                    placed(i + 1, 2)
                if finish:
                    scaled(i - 1, i - 1 + B)

            def heads_ahead(u):
                if u == 2:
                    heads_normalised(0)
                if u == 4:
                    heads_bias(0)
                if u == 10:
                    split(0)

            def heads_beside(u):
                if u == 6:
                    finish_normalised(B - 1)
                if u == 14:
                    scaled(B - 1, 2 * B - 1)

            feed_forward(0)
            for g in range(G - 1):
                placed(0, g)
            heads_batch(0, False, True)
            with pool.Fori(1, B - 1) as i:
                heads_batch(i, True, True)
            heads_batch(B - 1, True, False)
            feed_forward(B)

        @block.tensor
        def _(pe):
            pe.wait_ge(m["early_loaded"], 16 * N_EARLY)

            def transposes(to, src, rows_out=P):
                for t in range(T):
                    last = pe.transpose(to[0:rows_out, t * P:(t + 1) * P], src[:, t, :], ident[:, :])
                return last

            def by_tile(to, columns, w):
                for t in range(T):
                    last = pe.matmul(to[:, t * P:(t + 1) * P], columns[:, t * P:(t + 1) * P], w, start=True, stop=True)
                return last

            def logits(n, to):
                pe.wait_ge(m["xt2_ready"], n + 1)
                for t in range(T):
                    last = pe.matmul(to[:, t * NE:(t + 1) * NE], xt["ff"][:, t * P:(t + 1) * P], rws[:, :], start=True, stop=True)
                last.then_inc(m["logit_ps"], 1)

            def chunks_columns(i):
                pe.wait_ge(m["normed"], i + 1)
                transposes(bank[0], xn["in"]).then_inc(m["xt_ps"], 1)

            def chunks_queries(i):
                pe.wait_ge(m["xt_ready"], i + 1)
                if not at_first(i):
                    pe.wait_ge(m["v_ready"], i)
                pe.matmul(bank[1][:, :], wq[:, :], xt["in"][:, :], start=True, stop=True).then_inc(m["q_ps"], 1)

            def chunks_keys(i):
                pe.matmul(bank[0][:, :], wk[:, :], xt["in"][:, :], start=True, stop=True).then_inc(m["k_ps"], 1)

            def chunks_values(i):
                by_tile(bank[1], xt["in"], wv[:, :]).then_inc(m["v_ps"], 1)

            def chunks_scores(i, t):
                if not at_first(i):
                    pe.wait_ge(m["shift_done"], i * T + t + 1 - T)
                pe.matmul(bank[4 + t][:, :], qt[:, t * P:(t + 1) * P], kt[:, :], start=True, stop=True).then_inc(m["s_ps"], 1)

            def attention_columns(i, to=bank[2]):
                pe.wait_ge(m["abd_ready"], i * T + T)
                if not at_first(i):
                    pe.wait_ge(m["lg_ready"], i)
                transposes(to, abd).then_inc(m["abd_ps"], 1)

            def combined(i, to=bank[3]):
                pe.wait_ge(m["abdt_ready"], i + 1)
                pe.wait_ge(m["v_ready"], i + 1)
                for t in range(T):
                    last = pe.matmul(to[:, t * P:(t + 1) * P], v[:, t, :], tcol[:, t * P:(t + 1) * P], start=True, stop=True)
                last.then_inc(m["c_ps"], 1)

            def chunks_out(i, to=bank[2]):
                pe.wait_ge(m["ct_ready"], i + 1)
                by_tile(to, ccol, wo[:, :]).then_inc(m["o_ps"], 1)

            def routed_columns(i, to):
                pe.wait_ge(m["normed2"], i + 1)
                transposes(to, xn["ff"]).then_inc(m["xt2_ps"], 1)

            def chunks_batch(i, before, after):
                pe.wait_ge(m["qt_ready"], i + 1)
                pe.wait_ge(m["kt_ready"], i + 1)
                chunks_scores(i, 0)
                chunks_scores(i, 1)
                if before:
                    attention_columns(i - 1)
                chunks_scores(i, 2)
                if before:
                    combined(i - 1)
                chunks_scores(i, 3)
                chunks_values(i)
                if before:
                    chunks_out(i - 1)
                if after:
                    chunks_columns(i + 1)
                if after:
                    chunks_queries(i + 1)
                    chunks_keys(i + 1)
                if before:
                    routed_columns(i - 1, bank[3])
                    logits(i - 1, bank[2])

            chunks_columns(0)
            chunks_queries(0)
            chunks_keys(0)
            chunks_batch(0, False, True)
            pe.wait_ge(m["w_loaded"], 16 * N_CONST)
            pe.wait_ge(m["rws_ready"], 1)
            with pe.Fori(1, B - 1) as i:
                chunks_batch(i, True, True)
            chunks_batch(B - 1, True, False)

            def chunks_beside(u):
                if u == 0:
                    attention_columns(B - 1, bank[7])
                if u == 2:
                    combined(B - 1, bank[7])
                if u == 3:
                    chunks_out(B - 1, bank[7])
                if u == 8:
                    routed_columns(B - 1, bank[7])
                if u == 9:
                    pe.wait_ge(m["xcols_ready"], B)
                    logits(B - 1, bank[7])

            side = [None]

            def side_free():
                if side[0] is not None:
                    pe.wait_ge(m[side[0][0]], side[0][1])

            def side_used(name, count):
                side[0] = (name, count)

            def three(to, w0, high, low, start, stop):
                pe.matmul(to, wh[:, w0:w0 + P], high, start=start, stop=False)
                pe.matmul(to, wh[:, w0:w0 + P], low, start=False, stop=False)
                return pe.matmul(to, wl[:, w0:w0 + P], high, start=False, stop=stop)

            def ff_weight_columns(n):
                pe.wait_ge(m["combc_ready"], n + 1)
                transposes(bank[7], combc, 2 * NE).then_inc(m["comb_ps"], 1)

            def ff_down(n, u):
                pe.wait_ge(m["actl_done"], n * UNITS + u + 1)
                three(bank[6][:, :], (2 * UNITS + u) * P, acth[:, u % ACTS, :], actl[:, u % ACTS, :],
                      u == 0, u == UNITS - 1).then_inc(m["down"], 1)

            def ff_out(n):
                pe.wait_ge(m["ocol_ready"], n + 1)
                for t in range(T):
                    last = pe.transpose(bank[7][:, t * P:(t + 1) * P], ocol[:, t * P:(t + 1) * P], ident[:, :])
                last.then_inc(m["ot_ps"], 1)

            def ff_batch(n, i, parity, before, after, beside):
                pe.wait_ge(m["xl_ready"], n + 1)
                for u in range(UNITS):
                    if u >= 2 or before:
                        pe.wait_ge(m["prod_done"], n * UNITS + u - 1)
                    high, low = xh[:, parity, :], xl[:, parity, :]
                    three(bank[u % 2][:, :], u * P, high, low, True, True)
                    three(bank[2 + u % 2][:, :], (UNITS + u) * P, high, low, True, True).then_inc(m["gates"], 1)
                    if u % 2 == 0:
                        if u == 0:
                            pe.wait_ge(m["combt_ready"], n + 1)
                        if u >= 4 or before:
                            pe.wait_ge(m["act_done"], n * UNITS + u - 2)
                        pe.matmul(bank[4 + (u // 2) % 2][:, :], pickr[:, u // 2:u // 2 + 1].to_broadcast([2 * NE, P]), combt[:, :],
                                  start=True, stop=True).then_inc(m["cb_ps"], 1)
                    if u < AHEAD and before:
                        ff_down(n - 1, UNITS + u - AHEAD)
                    if u >= AHEAD:
                        if u == AHEAD and before:
                            pe.wait_ge(m["ocol_ready"], n)
                        ff_down(n, u - AHEAD)
                    if u == AHEAD + 1 and before:
                        ff_out(n - 1)
                    if u == 11 and after:
                        if before:
                            pe.wait_ge(m["res_f"], n)
                        else:
                            pe.wait_ge(m["lg_ready"], n + B)
                        ff_weight_columns(n + 1)
                    if beside:
                        beside(u)

            def feed_forward(first):
                if first == 0:
                    pe.wait_ge(m["wl_ready"], B - 2)
                    pe.wait_ge(m["consts_ready"], 1)
                    pe.wait_ge(m["shift_done"], B * T)
                    pe.wait_ge(m["v_ready"], B)
                    pe.wait_ge(m["lg_ready"], B - 1)
                else:
                    pe.wait_ge(m["sc_max"], B * H * T)
                    pe.wait_ge(m["st_exp"], B * STEPS * 2)
                    pe.wait_ge(m["ov_ready"], B * G)
                    side_free()
                ff_weight_columns(first)
                if first == B:
                    side_used("combt_ready", first + 1)
                over_batches(pe, first, ff_batch, *besides(first, chunks_beside, heads_ahead, heads_beside))
                n = first + B - 1
                for u in range(UNITS - AHEAD, UNITS):
                    ff_down(n, u)
                if first == 0:
                    side_free()
                ff_out(n)
                pe.wait_ge(m["res_f"], n + 1)
            def place_rows(b, g, part):
                side_free()
                hi, lo = ((qh, ql), (kh, kl))[part]
                pe.wait_ge(m["ql_ready"], b * 2 + part + 1)
                pe.matmul(bank[7][:, :], placer[:, 2 * part, g, :], hi[:, :], start=True, stop=False)
                pe.matmul(bank[7][:, :], placer[:, 2 * part + 1, g, :], lo[:, :], start=False, stop=True).then_inc(m["qp_ps"], 1)
                side_used(("qp_ready", "krow_ready")[part], b * G + g + 1)

            def score(i, at, hh):
                g, t = at // T % G, at % T
                n = i * (H * T) + at * GH + hh
                if not (at_first(i) and at * GH + hh < 2):
                    pe.wait_ge(m["sc_max"], n - 1)
                pe.matmul(bank[hh % 2][:, :], qp[:, g, t * P:(t + 1) * P], kp[:, hh, g, :],
                          start=True, stop=True).then_inc(m["sc_ps"], 1)

            def max_rows(b, g):
                side_free()
                pe.wait_ge(m["mpad_ready"], b * G + g + 1)
                pe.matmul(bank[7][:, :], identr[:, :], qp[:, g, :], start=True, stop=False)
                for t in range(T):
                    last = pe.matmul(bank[7][:, t * P:(t + 1) * P], mpad[:, t, :, :].rearrange("p h c -> p (h c)"), identr[:, :],
                                     start=False, stop=t == T - 1)
                last.then_inc(m["qpm_ps"], 1)
                side_used("qpm_ready", b * G + g + 1)

            def keys(i, s, hh):
                g, t, pair = s // T, s % T, hh // 2
                if hh % 2 == 0 and not (at_first(i) and s == 0):
                    pe.wait_ge(m["st_exp"], (i * STEPS + s) * 2 + pair - 1)
                last = pe.matmul(bank[KEY_BANKS[pair] + hh % 2][:, :], kp[:, hh, g, t * P:(t + 1) * P], qpm[:, g % 2, :],
                                 start=True, stop=True)
                if hh % 2:
                    last.then_inc(m["st_ps"], 1)

            def values(i, s):
                g, t = s // T % G, s % T
                pe.wait_ge(m["st_exp"], (i * STEPS + s) * 2 + 2)
                if t == 0 and not (at_first(i) and s == 0):
                    pe.wait_ge(m["ov_ready"], i * G + s // T)
                for hh in range(GH):
                    n = 2 * s + hh // 2
                    last = pe.matmul(bank[6][32 * hh:32 * hh + 32, :], va[:, t, g * GH + hh, :],
                                     eb[:, n % EBUFS, (hh % 2) * S:(hh % 2 + 1) * S], start=t == 0, stop=t == T - 1,
                                     tile_position=(0, 32 * hh))
                last.then_inc(m["pv_done"], 1)

            def to_rows(b, g):
                side_free()
                pe.wait_ge(m["ov_ready"], b * G + g + 1)
                for t in range(T):
                    last = pe.transpose(bank[7][:, t * P:(t + 1) * P], ov[:, t * P:(t + 1) * P], ident[:, :])
                last.then_inc(m["on_ps"], 1)
                side_used("on_ready", b * G + g + 1)

            def group_placed(b, g):
                pe.wait_ge(m["qp_ready"], b * G + g + 1)
                pe.wait_ge(m["kp_ready"], (b * G + g + 1) * GH)

            def finish_at(b, at):
                if at == (1, 0):
                    to_rows(b, G - 1)
                if at == (3, 0):
                    side_free()
                    pe.wait_ge(m["on_ready"], b * G + G)
                    transposes(bank[7], on).then_inc(m["ont_ps"], 1)
                    side_used("ont_ready", b + 1)
                if at == (4, 0):
                    side_free()
                    pe.wait_ge(m["ont_ready"], b + 1)
                    by_tile(bank[7], ccol, wfc[:, :]).then_inc(m["fc_ps"], 1)
                    side_used("res_b", b + 1)
                if at == (10, 0):
                    side_free()
                    pe.wait_ge(m["normed2"], b + B + 1)
                    transposes(bank[7], xn["ff"]).then_inc(m["xt2_ps"], 1)
                    side_used("xcols_ready", b + B + 1)
                if at == (11, 0):
                    side_free()
                    logits(b + B, bank[7])
                    side_used("lg_ready", b + B + 1)

            def prepare_at(b, at):
                if at == (3, 1):
                    side_free()
                    pe.wait_ge(m["bnormed"], b + 1)
                    transposes(bank[7], xn["in"]).then_inc(m["bxt_ps"], 1)
                    side_used("bxt_ready", b + 1)
                if at in ((4, 1), (5, 1)):
                    side_free()
                    pe.wait_ge(m["bxt_ready"], b + 1)
                    n = at[0] - 4
                    pe.matmul(bank[7][:, :], (wqb, wkb)[n][:, :], xt["in"][:, :], start=True, stop=True).then_inc(m["bqkv_ps"], 1)
                    side_used("qv_ready", b * 2 + n + 1)
                if at == (6, 0):
                    side_free()
                    by_tile(bank[7], xt["in"], wvb[:, :]).then_inc(m["bqkv_ps"], 1)
                    side_used("vb_ready", b + 1)
                if at in PLACED:
                    place_rows(b, *PLACED[at])

            def heads_batch(i, finish, prepare):
                for at in ((s, half) for s in range(STEPS) for half in range(2)):
                    s, half = at
                    ahead = s + LEAD < STEPS or prepare
                    if half == 0 and (s + LEAD) % T == 0 and ahead:
                        group_placed(i, (s + LEAD) // T)
                    if half == 0 and s % T == 0:
                        pe.wait_ge(m["qpm_ready"], i * G + s // T + 1)
                        pe.wait_ge(m["va_ready"], i * G + s // T + 1)
                    for hh in (2 * half, 2 * half + 1):
                        if ahead:
                            score(i, s + LEAD, hh)
                        keys(i, s, hh)
                    if half == 0 and (s >= 1 or finish):
                        values(i, s - 1)
                    if at in ((5, 0), (9, 0), (13, 0)):
                        to_rows(i, s // T - 1)
                    if finish:
                        finish_at(i - 1, at)
                    if at in LATE:
                        place_rows(i, G - 1, half)
                    if prepare:
                        prepare_at(i + 1, at)
                    if at in ((2, 1), (6, 1), (10, 1)):
                        max_rows(i, s // T + 1)
                    if at == (14, 1) and prepare:
                        max_rows(i + 1, 0)

            def heads_ahead(u):
                if u == 6:
                    side_used("res_f", B - 1)
                if u in (6, 7, 8, 9):
                    prepare_at(0, {6: (3, 1), 7: (4, 1), 8: (5, 1), 9: (6, 0)}[u])

            def heads_beside(u):
                if u in (0, 3, 5, 9, 10):
                    finish_at(B - 1, {0: (1, 0), 3: (3, 0), 5: (4, 0), 9: (10, 0), 10: (11, 0)}[u])

            feed_forward(0)
            pe.wait_ge(m["placer_ready"], 1)
            pe.wait_ge(m["ones_ready"], 1)
            side[0] = None
            for at in PLACED:
                prepare_at(0, at)
            for k in range(LEAD):
                if k % T == 0:
                    group_placed(0, k // T)
                for hh in range(GH):
                    score(0, k, hh)
            max_rows(0, 0)
            heads_batch(0, False, True)
            with pe.Fori(1, B - 1) as i:
                side_used("qpm_ready", i * G + 1)
                heads_batch(i, True, True)
            side_used("qpm_ready", (B - 1) * G + 1)
            heads_batch(B - 1, True, False)
            values(B - 1, STEPS - 1)
            feed_forward(B)


_INS = ("x", "wq", "wk", "wv", "wo", "wqb", "wkb", "wvb", "wfc", "cols", "rows", "rw", "pes", "wgate", "wdown",
        "ident", "own", "block_mask", "iota", "place", "pick")


def kernel(L0_attn_a_x, L0_attn_a_Wq, L0_attn_a_bq, L0_attn_a_Wk, L0_attn_a_bk, L0_attn_a_Wv, L0_attn_a_bv, L0_attn_a_Wo,
           L0_attn_a_bo, L0_attn_b_head_mask, L0_attn_b_qkv_w, L0_attn_b_qkv_b, L0_attn_b_fc_w, L0_attn_b_fc_b,
           L0_ffn_router_scale, L0_ffn_router_w, L0_ffn_gating_w, L0_ffn_linear_w, L0_ffn_per_expert_scale):
    import numpy as np
    import concourse.bacc as bacc
    from concourse.bass_utils import run_bass_kernel_spmd

    A = np.asarray
    qkv = A(L0_attn_b_qkv_w).reshape(H, 3, HD, P)
    qkvb = A(L0_attn_b_qkv_b).reshape(H, 3, HD)
    mask = np.repeat(A(L0_attn_b_head_mask), HD)
    p = np.arange(P)
    own = np.where(np.arange(NC)[None, None, :] == np.arange(T)[None, :, None] * T + p[:, None, None] // CHUNK, 2, 1)
    block_mask = np.broadcast_to(np.arange(T)[None, :, None] == p[:, None, None] // CHUNK, (P, T, CHUNK))
    one_rows = (p % 32 == ONE) | (p % 32 == ONE + 1)
    of_head = [p // 32 == h for h in range(GH)]
    place = np.zeros((P, 4, G, P), np.float32)
    for part, copies in enumerate(((0, 1), (2,), (0, 2), (1,))):
        for c in copies:
            for h in range(H):
                for j in range(HD):
                    place[h * HD + j, part, h // GH, h % GH * 32 + c * HD + j] = 1
    pick = np.arange(2 * NE)[:, None] % NE == np.arange(NE)[None, :]
    arrays = {
        "x": A(L0_attn_a_x).reshape(B * S, P), "wq": A(L0_attn_a_Wq), "wk": A(L0_attn_a_Wk), "wv": A(L0_attn_a_Wv), "wo": A(L0_attn_a_Wo),
        "wqb": qkv[:, 0].reshape(P, P).T, "wkb": qkv[:, 1].reshape(P, P).T, "wvb": qkv[:, 2].reshape(P, P).T,
        "wfc": A(L0_attn_b_fc_w).T,
        "cols": np.stack([A(L0_attn_a_bq), A(L0_attn_a_bk), qkvb[:, 0].reshape(P), qkvb[:, 1].reshape(P), mask,
                          A(L0_ffn_router_scale)] + [a.astype(np.float32) for a in of_head + [one_rows]], 1),
        "rows": np.stack([A(L0_attn_a_bv), A(L0_attn_a_bo), qkvb[:, 2].reshape(P), A(L0_attn_b_fc_b), mask]),
        "rw": A(L0_ffn_router_w), "pes": A(L0_ffn_per_expert_scale),
        "wgate": A(L0_ffn_gating_w).transpose(3, 1, 0, 2).reshape(P, 2 * UNITS * P),
        "wdown": A(L0_ffn_linear_w).reshape(UNITS, P, P).transpose(1, 0, 2).reshape(P, UNITS * P),
        "ident": np.eye(P, dtype=np.float32), "own": own.astype(np.float32), "block_mask": block_mask.astype(np.float32),
        "iota": np.broadcast_to(np.arange(NE, dtype=np.float32), (P, NE)), "place": place, "pick": pick.astype(np.float32),
    }
    nc = bacc.Bacc("TRN2", target_bir_lowering=False, num_devices=1)
    sent, d = {}, {}
    for name in _INS:
        a = np.ascontiguousarray(arrays[name])
        sent[f"in_{name}"] = a
        d[name] = nc.dram_tensor(f"in_{name}", a.shape, mybir.dt.from_np(a.dtype), kind="ExternalInput").ap()
    out = nc.dram_tensor("out", (B * S, P), F32, kind="ExternalOutput").ap()
    build(nc, d, out)
    r = run_bass_kernel_spmd(nc, [sent], core_ids=[0])
    return r.results[0]["out"].reshape(B, S, P)
```
